# Optimizing a Trainium2 kernel written in Bass

```python
import numpy as np
import jax
import jax.numpy as jnp

def _softmax(x, axis=-1):
    return jax.nn.softmax(x, axis=axis)

def _gelu(x):
    return jax.nn.gelu(x, approximate=True)

def _silu(x):
    return jax.nn.silu(x)

def _sigmoid(x):
    return jax.nn.sigmoid(x)

def _layernorm(x, axis=-1, eps=1e-05):
    m = jnp.mean(x, axis=axis, keepdims=True)
    v = jnp.var(x, axis=axis, keepdims=True)
    return (x - m) / jnp.sqrt(v + eps)

def _scatter_add(tgt, idx, src, axis=0):
    return tgt.at[idx].add(src)

def _segment_sum(src, seg, n):
    return jax.ops.segment_sum(src, seg, n)
kernel_name = 'mk_adaln_d1_jaxref_r8_046fdc'

def setup_inputs(seed: int=0):
    np.random.seed(seed)
    _w = jnp.asarray

    def _L0_attn_setup():
        import jax, jax.numpy as jnp
        import numpy as np
        H = 512
        NH = 32
        QR = 192
        KVR = 64
        RD = 64
        ND = 128
        VD = 128
        QK = RD + ND
        EPS = 1e-06
        THETA = 10000.0
        B, S = (2, 128)

        def rmsnorm(x, w):
            norm = jnp.sqrt(jnp.sum(x * x, axis=-1, keepdims=True)) * x.shape[-1] ** (-0.5)
            return x / (norm + EPS) * w

        def rope_cos_sin(seq_len):
            inv_freq = 1.0 / THETA ** (jnp.arange(0, RD, 2, dtype=jnp.float32) / RD)
            t = jnp.arange(seq_len, dtype=jnp.float32)
            freqs = jnp.outer(t, inv_freq)
            emb = jnp.concatenate([freqs, freqs], -1)
            return (jnp.cos(emb), jnpp_cos_sin_dummy() if False else jnp.sin(emb))

        def rotate_half(x):
            x1, x2 = jnp.split(x, 2, axis=-1)
            return jnp.concatenate([-x2, x1], axis=-1)
        key = jax.random.key(seed)
        ks = jax.random.split(key, 8)
        sc = 0.02
        return {'hidden_states': jax.random.normal(ks[0], (B, S, H), jnp.float32), 'w_qa': jax.random.normal(ks[1], (H, QR), jnp.float32) * sc, 'g_qa': jnp.ones((QR,), jnp.float32), 'w_qb': jax.random.normal(ks[2], (QR, NH * QK), jnp.float32) * sc, 'w_kva': jax.random.normal(ks[3], (H, KVR + RD), jnp.float32) * sc, 'g_kva': jnp.ones((KVR,), jnp.float32), 'w_kvb': jax.random.normal(ks[4], (KVR, NH * (ND + VD)), jnp.float32) * sc, 'w_o': jax.random.normal(ks[5], (NH * VD, H), jnp.float32) * sc}
    _L0_attn_in = _L0_attn_setup()

    def _L0_ffn_setup():
        import jax, jax.numpy as jnp
        import numpy as np
        B_, S, D_IN, D_OUT = (4, 256, 512, 512)
        N, RANK, ALPHA = (8, 16, 32)
        SCALE = ALPHA / RANK
        key = jax.random.key(seed)
        kx, ka, kb, kw, kbias = jax.random.split(key, 5)
        x = jax.random.normal(kx, (B_, S, D_IN), dtype=jnp.float32)
        lora_A = jax.random.normal(ka, (N, RANK, D_IN), dtype=jnp.float32) * (1.0 / np.sqrt(D_IN))
        lora_B = jax.random.normal(kb, (N, D_OUT, RANK), dtype=jnp.float32) * (1.0 / np.sqrt(RANK))
        W = jax.random.normal(kw, (D_OUT, D_IN), dtype=jnp.float32) * (1.0 / np.sqrt(D_IN))
        bias = jax.random.normal(kbias, (D_OUT,), dtype=jnp.float32) * 0.01
        lora_weights = jnp.full((N,), 1.0 / N, dtype=jnp.float32)
        return {'x': x, 'lora_A': lora_A, 'lora_B': lora_B, 'W': W, 'bias': bias, 'lora_weights': lora_weights}
    _L0_ffn_in = _L0_ffn_setup()
    _L0_c = _w((lambda *s: np.random.randn(*s).astype(np.float32) * 0.05)(2, 512))
    _L0_wmod = _w((lambda *s: np.random.randn(*s).astype(np.float32) * 0.05)(512, 6 * 512) * 512 ** (-0.5))
    _d = {'L0_attn_hidden_states': _L0_attn_in['hidden_states'], 'L0_attn_w_qa': _L0_attn_in['w_qa'], 'L0_attn_g_qa': _L0_attn_in['g_qa'], 'L0_attn_w_qb': _L0_attn_in['w_qb'], 'L0_attn_w_kva': _L0_attn_in['w_kva'], 'L0_attn_g_kva': _L0_attn_in['g_kva'], 'L0_attn_w_kvb': _L0_attn_in['w_kvb'], 'L0_attn_w_o': _L0_attn_in['w_o'], 'L0_ffn_lora_A': _L0_ffn_in['lora_A'], 'L0_ffn_lora_B': _L0_ffn_in['lora_B'], 'L0_ffn_W': _L0_ffn_in['W'], 'L0_ffn_bias': _L0_ffn_in['bias'], 'L0_ffn_lora_weights': _L0_ffn_in['lora_weights'], 'L0_c': _L0_c, 'L0_wmod': _L0_wmod}
    _x0 = _d['L0_attn_hidden_states']
    _d['L0_attn_hidden_states'] = jax.random.normal(jax.random.fold_in(jax.random.key(seed), 1), (2, 512, 512), dtype=_x0.dtype)
    del _x0
    return _d

def reference(L0_attn_hidden_states, L0_attn_w_qa, L0_attn_g_qa, L0_attn_w_qb, L0_attn_w_kva, L0_attn_g_kva, L0_attn_w_kvb, L0_attn_w_o, L0_ffn_lora_A, L0_ffn_lora_B, L0_ffn_W, L0_ffn_bias, L0_ffn_lora_weights, L0_c, L0_wmod):

    def _L0_attn_ref(hidden_states, w_qa, g_qa, w_qb, w_kva, g_kva, w_kvb, w_o):
        import jax, jax.numpy as jnp
        import numpy as np
        H = 512
        NH = 32
        QR = 192
        KVR = 64
        RD = 64
        ND = 128
        VD = 128
        QK = RD + ND
        EPS = 1e-06
        THETA = 10000.0
        B, S = (2, 128)

        def rmsnorm(x, w):
            norm = jnp.sqrt(jnp.sum(x * x, axis=-1, keepdims=True)) * x.shape[-1] ** (-0.5)
            return x / (norm + EPS) * w

        def rope_cos_sin(seq_len):
            inv_freq = 1.0 / THETA ** (jnp.arange(0, RD, 2, dtype=jnp.float32) / RD)
            t = jnp.arange(seq_len, dtype=jnp.float32)
            freqs = jnp.outer(t, inv_freq)
            emb = jnp.concatenate([freqs, freqs], -1)
            return (jnp.cos(emb), jnpp_cos_sin_dummy() if False else jnp.sin(emb))

        def rotate_half(x):
            x1, x2 = jnp.split(x, 2, axis=-1)
            return jnp.concatenate([-x2, x1], axis=-1)
        b, s, _ = hidden_states.shape
        q_c = rmsnorm(hidden_states @ w_qa, g_qa)
        q = (q_c @ w_qb).reshape(b, s, NH, QK).transpose(0, 2, 1, 3)
        q_nope, q_rope = (q[..., :ND], q[..., ND:])
        kv = hidden_states @ w_kva
        k_c, k_rope = (kv[..., :KVR], kv[..., KVR:])
        k_c = rmsnorm(k_c, g_kva)
        kst = (k_c @ w_kvb).reshape(b, s, NH, ND + VD).transpose(0, 2, 1, 3)
        k_nope, v = (kst[..., :ND], kst[..., ND:])
        inv_freq = 1.0 / THETA ** (jnp.arange(0, RD, 2, dtype=jnp.float32) / RD)
        freqs = jnp.outer(jnp.arange(s, dtype=jnp.float32), inv_freq)
        emb = jnp.concatenate([freqs, freqs], -1)
        cos = jnp.cos(emb)[None, None]
        sin = jnp.sin(emb)[None, None]
        k_rope = k_rope[:, None]
        q_rope = q_rope * cos + rotate_half(q_rope) * sin
        k_rope = k_rope * cos + rotate_half(k_rope) * sin
        k_rope = jnp.broadcast_to(k_rope, (b, NH, s, RD))
        query = jnp.concatenate([q_nope, q_rope], -1)
        key_s = jnp.concatenate([k_nope, k_rope], -1)
        scaling = QK ** (-0.5)
        scores = jnp.einsum('bhqd,bhkd->bhqk', query, key_s) * scaling
        attn = jax.nn.softmax(scores, axis=-1)
        out = jnp.einsum('bhqk,bhkd->bhqd', attn, v)
        out = out.transpose(0, 2, 1, 3).reshape(b, s, NH * VD)
        return out @ w_o

    def _L0_ffn_ref(x, lora_A, lora_B, W, bias, lora_weights):
        import jax, jax.numpy as jnp
        import numpy as np
        B_, S, D_IN, D_OUT = (4, 256, 512, 512)
        N, RANK, ALPHA = (8, 16, 32)
        SCALE = ALPHA / RANK
        h = jnp.einsum('bsd,nrd->nbsr', x, lora_A)
        coef = (SCALE * lora_weights)[:, None, None]
        lora_out = jnp.einsum('nbsr,nor->bso', h, lora_B * coef)
        base = jnp.einsum('bsd,od->bso', x, W) + bias
        return base + lora_out
    x = L0_attn_hidden_states
    mod = (_silu(L0_c) @ L0_wmod).reshape(L0_c.shape[0], 6, 1, -1)
    sa, ca, ga, sb, cb, gb = (mod[:, 0], mod[:, 1], mod[:, 2], mod[:, 3], mod[:, 4], mod[:, 5])
    ga = (2 * (ga >= 0) - 1) * jnp.maximum(jnp.abs(ga), 0.25)
    gb = (2 * (gb >= 0) - 1) * jnp.maximum(jnp.abs(gb), 0.25)
    h = _layernorm(x, axis=-1) * (1 + ca) + sa
    x = x + ga * _L0_attn_ref(h, L0_attn_w_qa, L0_attn_g_qa, L0_attn_w_qb, L0_attn_w_kva, L0_attn_g_kva, L0_attn_w_kvb, L0_attn_w_o)
    h = _layernorm(x, axis=-1) * (1 + cb) + sb
    x = x + gb * _L0_ffn_ref(h, L0_ffn_lora_A, L0_ffn_lora_B, L0_ffn_W, L0_ffn_bias, L0_ffn_lora_weights)
    return x

_drawn_inputs = setup_inputs


def setup_inputs(seed=0):
    import zlib

    import numpy as np

    out = dict(_drawn_inputs(seed))
    spreads = {'L0_attn_g_qa': (1.0, 0.6),
     'L0_attn_g_kva': (1.0, 0.6),
     'L0_ffn_lora_weights': (0.125, 0.6)}
    factors = {'L0_attn_w_qa': 8.0,
     'L0_attn_w_qb': 8.0,
     'L0_attn_w_kva': 8.0,
     'L0_attn_w_kvb': 8.0,
     'L0_attn_w_o': 8.0,
     'L0_ffn_bias': 64.0}
    for name, (base, spread) in spreads.items():
        noise = np.random.default_rng([zlib.crc32(name.encode()), seed]).standard_normal(out[name].shape)
        drawn = base * np.exp(spread * noise) if base else spread * noise
        out[name] = jnp.asarray(drawn.astype(out[name].dtype))
    for name, factor in factors.items():
        out[name] = (out[name] * factor).astype(out[name].dtype)
    return out
```

```python
from contextlib import ExitStack

import numpy as np

import concourse.bass as bass
from concourse import mybir

B, S, H = 2, 512, 512
NH = 32
QR, KVR, RD, ND, VD = 192, 64, 64, 128, 128
P = 128
QT = S // P
TT = B * QT
HC = H // P
QRB = QR - P
PAIRS = NH // 2
UNITS = 2 * B
TILES = UNITS * QT
LW = 2 * P + P
WQ_COLS = 2 * P + KVR
WO_COLS = P + H
SCALING = (ND + RD) ** -0.5
EPS_LN, EPS_RMS = 1e-5, 1e-6
SHIFT_A, SCALE_A, GATE_A, SHIFT_B, SCALE_B, GATE_B = range(6)

LEAD_LOAD_WQ = 32
LEAD_ABSORB = 27
LEAD_Q = 24
LEAD_S = 18
LEAD_EXP = 17
LEAD_T = 15
LEAD_LOW = 14
LEAD_LOAD_WO = 15
LEAD_VO = 5
LEAD_PV = 11
OUT_SLOTS = (1, 2, 3, 5, 6, 7, 9, 10)
RAMP = 2


def build(nc, x, w_lat, g_lat_q, g_lat_k, wq_pack, rope_pack, wo_pack, lora_a, lora_b, lora_w,
          w_ffn_t, bias, c_t, w_mod, ident_in, rope_q, rope_k, out):
    fp32 = mybir.dt.float32
    f32r = mybir.dt.float32r
    ALU = mybir.AluOpType
    ACT = mybir.ActivationFunctionType
    AX_X = mybir.AxisListType.X

    x_v = x.rearrange("b (t p) d -> p b t d", p=P)
    out_v = out.rearrange("b (t p) d -> p (b t) d", p=P)
    w_mod_v = w_mod.rearrange("(c p) (s n) -> s p c n", p=P, s=6)

    ctx = ExitStack()
    with ctx:
        def sb(name, shape, dt=fp32, where=ctx):
            return where.enter_context(nc.sbuf_tensor(name, shape, dt))

        def sem(name):
            return ctx.enter_context(nc.semaphore(name))

        xs = sb("xs", [P, TT, H])
        acc = sb("acc", [P, TT, H])
        h_t = sb("h_t", [P, B, HC, S])
        ident = sb("ident", [P, P])
        ropeq = sb("ropeq", [P, 2, S])
        ropek = sb("ropek", [P, 2, QT, RD])
        gq = sb("gq", [P, 2])
        gk = sb("gk", [P, KVR])
        gates = sb("gates", [P, 2, B, H])
        modc = sb("modc", [P, 4, HC, B])
        stats = sb("stats", [P, TT, 6])
        mv = sb("mv", [P, TT, 2])
        sd = sb("sd", [P, TT])
        rs = sb("rs", [P, TT])
        w_eff = sb("w_eff", [P, HC, H])
        bias_b = sb("bias_b", [P, H])
        kt_hi = sb("kt_hi", [P, B, S], f32r)
        kt_lo = sb("kt_lo", [P, B, S], f32r)
        kc = sb("kc", [P, B, QT, P], f32r)
        qa_hi = sb("qa_hi", [P, B, S], f32r)
        qa_lo = sb("qa_lo", [P, B, S], f32r)
        qb_hi = sb("qb_hi", [P, B, S], f32r)
        qb_lo = sb("qb_lo", [P, B, S], f32r)

        first = ExitStack()
        wm = sb("wm", [P, 3, HC, H], where=first)
        w_l = sb("w_l", [P, HC, LW], where=first)
        tok = sb("tok", [P, TT, LW], where=first)
        kp = sb("kp", [P, TT, P], where=first)
        c_col = sb("c_col", [P, HC, B], where=first)
        e_col = sb("e_col", [P, HC, B], where=first)
        s_col = sb("s_col", [P, HC, B], where=first)
        s_bc = sb("s_bc", [P, HC, B, P], where=first)
        first.close()

        pt_hi = sb("pt_hi", [P, 2, QT, S], f32r)
        pt_lo = sb("pt_lo", [P, 2, QT, S], f32r)
        x1 = sb("x1", [P, UNITS, S], f32r)
        x2 = sb("x2", [P, UNITS, S], f32r)
        m1 = sb("m1", [P, 2, H], f32r)
        m2 = sb("m2", [P, 2, H], f32r)
        probs = sb("probs", [P, 4, S])
        q_raw = sb("q_raw", [P, S])
        q_rot = sb("q_rot", [P, S])
        q_f = sb("q_f", [P, S])
        q_hi = sb("q_hi", [P, 2, S], f32r)
        q_lo = sb("q_lo", [P, 2, S], f32r)
        wq_in = sb("wq_in", [P, 2, WQ_COLS])
        w_f = sb("w_f", [P, 2, 2, P])
        wh = sb("wh", [P, 2, 2, P], f32r)
        wl = sb("wl", [P, 2, P], f32r)
        wo_in = sb("wo_in", [P, 2, WO_COLS])
        one = sb("one", [P, 1])
        neg_max = sb("neg_max", [P, 4])
        row_sum = sb("row_sum", [P, 4])
        row_rec = sb("row_rec", [P, 4])
        gate_abs = sb("gate_abs", [P, 2, B, H])
        lora_a_sb = sb("lora_a_sb", [P, H])
        lora_b_sb = sb("lora_b_sb", [P, H])
        lora_w_sb = sb("lora_w_sb", [P, 1])
        ssq = sb("ssq", [P, TT, 2])
        nrm = sb("nrm", [P, TT, 2])
        junk = gate_abs[:, :, :, :].rearrange("p k b (h n) -> p (k b h) n", h=2)
        k_rot = sb("k_rot", [P, QT, RD])

        ps = [ctx.enter_context(nc.psum_tensor(f"ps{i}", [P, S], fp32)) for i in range(8)]
        s_bank, t_bank = ps[0:2], ps[2:4]
        pv_bank, out_bank = ps[4:6], ps[6]
        work_bank = ps[7]

        ld_x = [sem(f"ld_x{b}") for b in range(B)]
        ld_ident, ld_c, ld_wl, ld_small, ld_lora = (sem(n) for n in ("ld_ident", "ld_c", "ld_wl", "ld_small", "ld_lora"))
        ld_mod = [sem(f"ld_mod{i}") for i in range(6)]
        ld_wq, ld_wo, rot_moved, stored = (sem(n) for n in ("ld_wq", "ld_wo", "rot_moved", "stored"))
        ve, pool_step = sem("ve"), sem("pool_step")
        var_ready, sd_ready, xn_ready, xt_done = (sem(n) for n in ("var_ready", "sd_ready", "xn_ready", "xt_done"))
        e_ready, silu_ready, silu_bc, modc_done, modc_ready = (
            sem(n) for n in ("e_ready", "silu_ready", "silu_bc", "modc_done", "modc_ready"))
        mod_used = [sem(f"mod_used{i}") for i in range(3)]
        ht_ready = [sem(f"ht_ready{b}") for b in range(B)]
        tok_done, tok_copied, ssq_ready, nrm_ready = (sem(n) for n in ("tok_done", "tok_copied", "ssq_ready", "nrm_ready"))
        kq_ready, kq_turned, kqt_hi, kqt_lo, kc_ready = (sem(n) for n in ("kq_ready", "kq_turned", "kqt_hi", "kqt_lo", "kc_ready"))
        gate_done, gate_copied, gates_ready, lora_b_ready, lora_done, w_eff_ready = (
            sem(n) for n in ("gate_done", "gate_copied", "gates_ready", "lora_b_ready", "lora_done", "w_eff_ready"))
        acc_zero, res_ready, ffn_done, y_biased, y_gated, y_ready = (
            sem(n) for n in ("acc_zero", "res_ready", "ffn_done", "y_biased", "y_gated", "y_ready"))
        xn2_ready, xt2_done, ht2_ready, var2_ready, sd2_ready = (
            sem(n) for n in ("xn2_ready", "xt2_done", "ht2_ready", "var2_ready", "sd2_ready"))
        absorbed, w_copied, wh_done, wl_ready, wb_ready, rot_clear = (
            sem(n) for n in ("absorbed", "w_copied", "wh_done", "wl_ready", "wb_ready", "rot_clear"))
        q_done, q_raw_ready, q_cos_ready, q_rotated, q_added, q_hi_ready, q_lo_ready = (
            sem(n) for n in ("q_done", "q_raw_ready", "q_cos_ready", "q_rotated", "q_added", "q_hi_ready", "q_lo_ready"))
        s_done, max_ready, exp_done, rec_ready, normed = (
            sem(n) for n in ("s_done", "max_ready", "exp_done", "rec_ready", "normed"))
        t_done, t_hi_ready, t_lo_ready, pv_done, x_hi_ready, x_lo_ready = (
            sem(n) for n in ("t_done", "t_hi_ready", "t_lo_ready", "pv_done", "x_hi_ready", "x_lo_ready"))
        vo_done, m_hi_ready, m_lo_ready, o_done, o_added = (
            sem(n) for n in ("vo_done", "m_hi_ready", "m_lo_ready", "o_done", "o_added"))

        block = ctx.enter_context(nc.Block())

        def item(it, slot, lead, per_step=TILES):
            ahead, local = divmod(slot + lead, per_step)
            step = it + ahead
            if isinstance(step, int) and not 0 <= step < PAIRS:
                return None
            return step, local

        def wait_count(eng, semaphore, count):
            if not isinstance(count, int) or count > 0:
                eng.wait_ge(semaphore, count)

        def run_steps(eng, step):
            for it in range(-RAMP, 0):
                step(it)
            with eng.Fori(0, PAIRS - RAMP) as it:
                step(it)
            for it in range(PAIRS - RAMP, PAIRS):
                step(it)

        def bank_left(eng, it, slot):
            wanted = {
                0: (m_lo_ready, 2, 2, 2 * PAIRS), 4: (q_cos_ready, UNITS, 7, UNITS * PAIRS),
                5: (q_cos_ready, UNITS, 8, UNITS * PAIRS), 8: (w_copied, 1, 3, PAIRS),
                11: (q_cos_ready, UNITS, 9, UNITS * PAIRS), 12: (m_lo_ready, 2, 3, 2 * PAIRS),
                14: (q_cos_ready, UNITS, 10, UNITS * PAIRS),
            }
            semaphore, per_step, ahead, most = wanted[slot]
            count = per_step * it + ahead
            wait_count(eng, semaphore, min(count, most) if isinstance(it, int) else count)

        def unit_of(tile):
            return tile // QT, tile % QT

        @block.sync
        def _(sp):
            sp.dma_start(ident[:, :], ident_in).then_inc(ld_ident, 16)
            sp.dma_start(xs[:, 0:QT, :], x_v[:, 0]).then_inc(ld_x[0], 16)
            sp.dma_start(c_col[:, :, :], c_t.rearrange("(c p) b -> p c b", p=P)).then_inc(ld_c, 16)
            sp.dma_start(wm[:, 0], w_mod_v[SCALE_A]).then_inc(ld_mod[SCALE_A], 16)
            sp.dma_start(wm[:, 1], w_mod_v[SHIFT_A]).then_inc(ld_mod[SHIFT_A], 16)
            sp.dma_start(w_l[:, :, :], w_lat.rearrange("(c p) n -> p c n", p=P)).then_inc(ld_wl, 16)
            sp.dma_start(xs[:, QT:TT, :], x_v[:, 1]).then_inc(ld_x[1], 16)
            sp.dma_start(ropek[:, :, :, :], rope_k).then_inc(ld_small, 16)
            sp.dma_start(ropeq[:, :, :], rope_q).then_inc(ld_small, 16)
            sp.dma_start(gq[:, :], g_lat_q).then_inc(ld_small, 16)
            sp.dma_start(gk[:, :], g_lat_k.partition_broadcast(P)).then_inc(ld_small, 16)
            sp.dma_start(bias_b[:, :], bias.partition_broadcast(P)).then_inc(ld_small, 16)
            sp.dma_start(wm[:, 2], w_mod_v[SCALE_B]).then_inc(ld_mod[SCALE_B], 16)
            sp.dma_start(lora_a_sb[:, :], lora_a).then_inc(ld_lora, 16)
            sp.dma_start(lora_b_sb[:, :], lora_b).then_inc(ld_lora, 16)
            sp.dma_start(lora_w_sb[:, :], lora_w).then_inc(ld_lora, 16)
            sp.dma_start(w_eff[:, :, :], w_ffn_t.rearrange("(c p) n -> p c n", p=P)).then_inc(ld_lora, 16)
            for buf, section in ((0, SHIFT_B), (1, GATE_A), (2, GATE_B)):
                sp.wait_ge(mod_used[buf], 1)
                sp.dma_start(wm[:, buf], w_mod_v[section]).then_inc(ld_mod[section], 16)

            def step(it):
                for slot in range(TILES):
                    at = item(it, slot, LEAD_LOAD_WQ)
                    if at and slot == 0:
                        g, _ = at
                        wait_count(sp, absorbed, g)
                        wait_count(sp, wl_ready, g)
                        wait_count(sp, wb_ready, g)
                        sp.dma_start(wq_in[:, :, :], wq_pack[g]).then_inc(ld_wq, 16)
                        for ab in range(2):
                            sp.dma_start(w_f[:, :, ab, KVR:P], rope_pack[g][:, :, ab]).then_inc(ld_wq, 16)
                    at = item(it, slot, LEAD_LOAD_WO)
                    if at and slot == 1:
                        g, _ = at
                        wait_count(sp, vo_done, 2 * g)
                        sp.dma_start(wo_in[:, :, :], wo_pack[g]).then_inc(ld_wo, 16)
                    at = item(it, slot, LEAD_Q)
                    if at and at[1] % QT == 0:
                        g, tile = at
                        n = UNITS * g + tile // QT
                        sp.wait_ge(q_raw_ready, n + 1)
                        sp.dma_start(q_rot[64:96, :], q_raw[96:128, :]).then_inc(rot_moved, 16)
                        sp.dma_start(q_rot[96:128, :], q_raw[64:96, :]).then_inc(rot_moved, 16)

            sp.wait_ge(rot_clear, 1)
            run_steps(sp, step)
            for tt in range(TT):
                sp.wait_ge(y_ready, tt + 1)
                sp.dma_start(out_v[:, tt, :], acc[:, tt, :]).then_inc(stored, 16)
            sp.wait_ge(stored, 16 * TT)

        @block.tensor
        def _(pe):
            mm = nc.tensor.matmul

            def turn_x(b, ready, count, done, banks):
                pe.wait_ge(ready, count)
                for c in range(HC):
                    for t in range(QT):
                        last = nc.tensor.transpose(banks[c][:, t * P:(t + 1) * P],
                                                   acc[:, QT * b + t, c * P:(c + 1) * P], ident[:, :])
                    last.then_inc(done, 1)

            def mod_columns(bank, place, buf, section):
                pe.wait_ge(ld_mod[section], 16)
                for n in range(HC):
                    col = (place * HC + n) * B
                    for k in range(HC):
                        last = mm(bank[:, col:col + B], wm[:, buf, k, n * P:(n + 1) * P], s_col[:, k, :],
                                  start=(k == 0), stop=(k == HC - 1))
                last.then_inc(mod_used[buf], 1)

            pe.wait_ge(ld_ident, 16)
            turn_x(0, xn_ready, QT, xt_done, ps[0:4])
            pe.wait_ge(silu_ready, 1)
            mod_columns(ps[7], 0, 0, SCALE_A)
            mod_columns(ps[7], 1, 1, SHIFT_A)
            pe.wait_ge(modc_ready, 1)
            turn_x(1, xn_ready, TT, xt_done, ps[4:8])
            pe.wait_ge(ld_wl, 16)
            for b in range(B):
                pe.wait_ge(ht_ready[b], HC)
                for t in range(QT):
                    tt = QT * b + t
                    for c in range(HC):
                        last = mm(ps[tt][:, 0:LW], h_t[:, b, c, t * P:(t + 1) * P], w_l[:, c, :],
                                  start=(c == 0), stop=(c == HC - 1))
                    last.then_inc(tok_done, 1)
            for b in range(B):
                pe.wait_ge(kq_ready, b + 1)
                for j in range(3):
                    for t in range(QT):
                        tt = QT * b + t
                        src = kp[:, tt, :] if j == 0 else tok[:, tt, (j - 1) * P:j * P]
                        last = nc.tensor.transpose(ps[QT * b + j][:, t * P:(t + 1) * P], src, ident[:, :])
                    last.then_inc(kq_turned, 1)
            mod_columns(ps[3], 0, 2, SCALE_B)
            mod_columns(ps[3], 1, 0, SHIFT_B)
            pe.wait_ge(silu_bc, 1)
            pe.wait_ge(kqt_lo, 3)
            for buf, section, kind in ((1, GATE_A, 0), (2, GATE_B, 1)):
                pe.wait_ge(ld_mod[section], 16)
                for b in range(B):
                    bank = (ps[0], ps[1], ps[2], ps[7])[2 * kind + b]
                    for k in range(HC):
                        last = mm(bank[:, :], s_bc[:, k, b, :], wm[:, buf, k, :], start=(k == 0), stop=(k == HC - 1))
                    last.then_inc(gate_done, 1)
            pe.wait_ge(lora_b_ready, 1)
            pe.wait_ge(kqt_lo, 6)
            pe.wait_ge(modc_ready, 2)
            for c in range(HC):
                mm(ps[3 + c][:, :], lora_a_sb[:, c * P:(c + 1) * P], lora_b_sb[:, :],
                   start=True, stop=True).then_inc(lora_done, 1)
            pe.wait_ge(gate_copied, 2 * 2 * B)
            pe.wait_ge(w_eff_ready, HC)
            pe.wait_ge(kc_ready, B)
            pe.nop().then_inc(o_done, 1)

            def step(it):
                for slot in range(TILES):
                    at = item(it, slot, LEAD_T)
                    if at:
                        g, tile = at
                        n = TILES * g + tile
                        pe.wait_ge(normed, n + 1)
                        wait_count(pe, t_hi_ready, n - 1)
                        wait_count(pe, t_lo_ready, n - 1)
                        for j in range(QT):
                            last = nc.tensor.transpose(t_bank[tile % 2][:, j * P:(j + 1) * P],
                                                       probs[:, tile % 4, j * P:(j + 1) * P], ident[:, :])
                        last.then_inc(t_done, 1)

                    at = item(it, slot, LEAD_S)
                    if at:
                        g, tile = at
                        n = TILES * g + tile
                        u, t = unit_of(tile)
                        if t == 0:
                            pe.wait_ge(q_hi_ready, UNITS * g + u + 1)
                            pe.wait_ge(q_lo_ready, UNITS * g + u + 1)
                        wait_count(pe, exp_done, n - 1)
                        bank, cols, b = s_bank[tile % 2], slice(t * P, (t + 1) * P), u // 2
                        mm(bank[:, :], q_lo[:, u % 2, cols], kt_hi[:, b, :], start=True, stop=False)
                        mm(bank[:, :], q_hi[:, u % 2, cols], kt_lo[:, b, :], start=False, stop=False)
                        mm(bank[:, :], q_hi[:, u % 2, cols], kt_hi[:, b, :], start=False,
                           stop=True).then_inc(s_done, 1)

                    if slot in OUT_SLOTS and item(it, slot, 0):
                        m = OUT_SLOTS.index(slot)
                        b, t = divmod(m, QT)
                        n = TT * it + m
                        if m == 0:
                            pe.wait_ge(m_hi_ready, 4 * it + 4)
                            pe.wait_ge(m_lo_ready, 2 * it + 2)
                        if t == 0:
                            pe.wait_ge(x_hi_ready, 2 * (UNITS * it + 2 * b + 2))
                            pe.wait_ge(x_lo_ready, UNITS * it + 2 * b + 2)
                        pe.wait_ge(o_added, 1 + n)
                        cols = slice(t * P, (t + 1) * P)
                        for hl in range(2):
                            u = 2 * b + hl
                            mm(out_bank[:, :], x2[:, u, cols], m2[:, hl, :], start=(hl == 0), stop=False)
                            last = mm(out_bank[:, :], x1[:, u, cols], m1[:, hl, :], start=False, stop=(hl == 1))
                        last.then_inc(o_done, 1)

                    at = item(it, slot, LEAD_ABSORB)
                    if at and at[1] == 0:
                        g, _ = at
                        pe.wait_ge(ld_wq, 48 * (g + 1))
                        bank_left(pe, it, slot)
                        for hl in range(2):
                            for ab in range(2):
                                col = (2 * hl + ab) * KVR
                                last = mm(work_bank[:, col:col + KVR], wq_in[:, hl, ab * P:(ab + 1) * P],
                                          wq_in[:, hl, 2 * P:WQ_COLS], start=True, stop=True)
                        last.then_inc(absorbed, 1)

                    for hl in range(2):
                        at = item(it, slot, LEAD_VO - 3 * hl)
                        if at and at[1] == 0:
                            g, _ = at
                            if hl == 0:
                                pe.wait_ge(ld_wo, 16 * (g + 1))
                            bank_left(pe, it, slot)
                            mm(work_bank[:, :], wo_in[:, hl, 0:P], wo_in[:, hl, P:WO_COLS],
                               start=True, stop=True).then_inc(vo_done, 1)

                    at = item(it, slot, LEAD_Q)
                    if at and at[1] % QT == 0:
                        g, tile = at
                        u, _ = unit_of(tile)
                        n = UNITS * g + u
                        b, hl = divmod(u, 2)
                        if u == 0:
                            pe.wait_ge(wl_ready, g + 1)
                            pe.wait_ge(wb_ready, g + 1)
                        bank_left(pe, it, slot)
                        wait_count(pe, q_cos_ready, n)
                        mm(work_bank[:, :], wl[:, hl, :], qa_hi[:, b, :], start=True, stop=False)
                        mm(work_bank[:, :], wh[:, hl, 0, :], qa_lo[:, b, :], start=False, stop=False)
                        mm(work_bank[:, :], wh[0:QRB, hl, 1, :], qb_lo[0:QRB, b, :], start=False, stop=False)
                        mm(work_bank[:, :], wh[:, hl, 1, :], qb_hi[:, b, :], start=False, stop=False)
                        mm(work_bank[:, :], wh[:, hl, 0, :], qa_hi[:, b, :], start=False,
                           stop=True).then_inc(q_done, 1)

                    at = item(it, slot, LEAD_PV)
                    if at:
                        g, tile = at
                        u, j = unit_of(tile)
                        n = UNITS * g + u
                        if j == 0:
                            pe.wait_ge(t_hi_ready, QT * n + QT)
                            pe.wait_ge(t_lo_ready, QT * n + QT)
                            wait_count(pe, x_hi_ready, 2 * (n - 1))
                            wait_count(pe, x_lo_ready, n - 1)
                        mm(pv_bank[u % 2][:, :], kc[:, u // 2, j, :], pt_lo[:, u % 2, j, :], start=(j == 0), stop=False)
                        last = mm(pv_bank[u % 2][:, :], kc[:, u // 2, j, :], pt_hi[:, u % 2, j, :],
                                  start=False, stop=(j == QT - 1))
                        if j == QT - 1:
                            last.then_inc(pv_done, 1)

            run_steps(pe, step)

            for b in range(B):
                if b:
                    pe.wait_ge(ht2_ready, HC * b)
                turn_x(b, xn2_ready, QT * (b + 1), xt2_done, ps[0:4])
                pe.wait_ge(ht2_ready, HC * (b + 1))
                if b == 0:
                    pe.wait_ge(o_added, 1 + TT * PAIRS)
                for t in range(QT):
                    n = QT * b + t
                    if n >= 4:
                        pe.wait_ge(y_biased, n - 3)
                    for c in range(HC):
                        last = mm(ps[4 + n % 4][:, :], h_t[:, b, c, t * P:(t + 1) * P], w_eff[:, c, :],
                                  start=(c == 0), stop=(c == HC - 1))
                    last.then_inc(ffn_done, 1)

        @block.vector
        def _(dve):
            v = nc.vector
            chain = [0]

            def link(ins):
                chain[0] += 1
                ins.then_inc(ve, 1)
                dve.wait_ge(ve, chain[0])

            def layer_norm(b, var_done, sd_done, xn_done):
                tiles = range(QT * b, QT * b + QT)
                for tt in tiles:
                    last = v.bn_stats(stats[:, tt, :], xs[:, tt, :])
                link(last)
                for tt in tiles:
                    last = v.bn_aggr(mv[:, tt, :], stats[:, tt, :])
                link(last)
                span = slice(QT * b, QT * b + QT)
                v.tensor_scalar(sd[:, span], mv[:, span, 1], EPS_LN, None, ALU.add).then_inc(var_done, 1)
                dve.wait_ge(sd_done, b + 1)
                link(v.reciprocal(rs[:, span], sd[:, span]))
                for tt in tiles:
                    v.tensor_scalar(acc[:, tt, :], xs[:, tt, :], mv[:, tt, 0:1], rs[:, tt:tt + 1],
                                    ALU.subtract, ALU.mult).then_inc(xn_done, 1)

            def modulate(b, c, bank, turned, count, kind, done):
                dve.wait_ge(turned, count)
                v.tensor_scalar(h_t[:, b, c, :], bank[:, :], modc[:, 2 * kind, c, b:b + 1],
                                modc[:, 2 * kind + 1, c, b:b + 1], ALU.mult, ALU.add).then_inc(done, 1)

            dve.wait_ge(ld_c, 16)
            dve.wait_ge(e_ready, 1)
            link(v.tensor_scalar(s_col[:, :, :], e_col[:, :, :], 1.0, None, ALU.add))
            link(v.reciprocal(e_col[:, :, :], s_col[:, :, :]))
            v.tensor_tensor(s_col[:, :, :], c_col[:, :, :], e_col[:, :, :], ALU.mult).then_inc(silu_ready, 1)
            dve.wait_ge(ld_x[0], 16)
            layer_norm(0, var_ready, sd_ready, xn_ready)
            dve.wait_ge(ld_x[1], 16)
            layer_norm(1, var_ready, sd_ready, xn_ready)
            dve.wait_ge(silu_ready, 1)
            v.tensor_copy(s_bc[:, :, :, :], s_col[:, :, :].unsqueeze(3).broadcast_to((P, HC, B, P))).then_inc(silu_bc, 1)
            dve.wait_ge(mod_used[1], 1)
            v.tensor_scalar(modc[:, 0], ps[7][:, 0:HC * B].rearrange("p (n b) -> p n b", b=B), 1.0, None, ALU.add)
            link(v.tensor_copy(modc[:, 1], ps[7][:, HC * B:2 * HC * B].rearrange("p (n b) -> p n b", b=B)))
            v.nop().then_inc(modc_ready, 1)
            for b in range(B):
                for c in range(2):
                    modulate(b, c, ps[4 * b + c], xt_done, HC * b + c + 1, 0, ht_ready[b])
            dve.wait_ge(ld_small, 16 * 5)
            for b in range(B):
                tiles = slice(QT * b, QT * b + QT)
                for t in range(QT):
                    tt = QT * b + t
                    dve.wait_ge(tok_done, tt + 1)
                    last = v.tensor_copy(tok[:, tt, :], ps[tt][:, 0:LW])
                last.then_inc(tok_copied, 1)
                dve.wait_ge(tok_copied, b + 1)
                kr = tok[:, tiles, 2 * P + KVR:LW]
                v.tensor_tensor(kp[:, tiles, KVR:P], kr, ropek[:, 0], ALU.mult)
                v.tensor_tensor(k_rot[:, :, 0:RD // 2], kr[:, :, RD // 2:RD], ropek[:, 1, :, 0:RD // 2], ALU.mult)
                link(v.tensor_tensor(k_rot[:, :, RD // 2:RD], kr[:, :, 0:RD // 2], ropek[:, 1, :, RD // 2:RD], ALU.mult))
                v.tensor_tensor(kp[:, tiles, KVR:P], kp[:, tiles, KVR:P], k_rot[:, :, :], ALU.add)
                dve.wait_ge(nrm_ready, b + 1)
                v.tensor_scalar(nrm[:, tiles, 0], nrm[:, tiles, 0], QR ** -0.5, EPS_RMS, ALU.mult, ALU.add)
                link(v.tensor_scalar(nrm[:, tiles, 1], nrm[:, tiles, 1], KVR ** -0.5, EPS_RMS, ALU.mult, ALU.add))
                link(v.reciprocal(ssq[:, tiles, :], nrm[:, tiles, :]))
                for tt in range(QT * b, QT * b + QT):
                    v.scalar_tensor_tensor(kp[:, tt, 0:KVR], tok[:, tt, 2 * P:2 * P + KVR], ssq[:, tt, 1:2],
                                           gk[:, :], ALU.mult, ALU.mult)
                for tt in range(QT * b, QT * b + QT):
                    last = v.tensor_scalar(tok[:, tt, 0:2 * P], tok[:, tt, 0:2 * P], ssq[:, tt, 0:1], None, ALU.mult)
                last.then_inc(kq_ready, 1)
                dve.wait_ge(kq_ready, b + 1)
                link(v.tensor_copy(kc[:, b, :, 0:KVR], kp[:, tiles, 0:KVR]))
                v.tensor_tensor(kc[:, b, :, KVR:P], kp[:, tiles, 0:KVR], kc[:, b, :, 0:KVR].bitcast(fp32),
                                ALU.subtract).then_inc(kc_ready, 1)
            for b in range(B):
                dve.wait_ge(kqt_hi, 3 * b + 1)
                v.tensor_tensor(kt_lo[:, b, :], ps[QT * b][:, :], kt_hi[:, b, :].bitcast(fp32),
                                ALU.subtract).then_inc(kqt_lo, 1)
                for j, (hi, lo) in enumerate(((qa_hi, qa_lo), (qb_hi, qb_lo))):
                    dve.wait_ge(kqt_hi, 3 * b + 2 + j)
                    v.scalar_tensor_tensor(lo[:, b, :], ps[QT * b + 1 + j][:, :], gq[:, j:j + 1],
                                           hi[:, b, :].bitcast(fp32), ALU.mult, ALU.subtract).then_inc(kqt_lo, 1)
            dve.wait_ge(mod_used[0], 2)
            v.tensor_scalar(modc[:, 2], ps[3][:, 0:HC * B].rearrange("p (n b) -> p n b", b=B), 1.0, None, ALU.add)
            link(v.tensor_copy(modc[:, 3], ps[3][:, HC * B:2 * HC * B].rearrange("p (n b) -> p n b", b=B)))
            v.nop().then_inc(modc_ready, 1)
            dve.wait_ge(ld_lora, 16 * 4)
            v.tensor_scalar(lora_b_sb[:, :], lora_b_sb[:, :], lora_w_sb[:, 0:1], 2.0, ALU.mult,
                            ALU.mult).then_inc(lora_b_ready, 1)
            for c in range(HC):
                dve.wait_ge(lora_done, c + 1)
                v.tensor_tensor(w_eff[:, c, :], ps[3 + c][:, :], w_eff[:, c, :], ALU.add).then_inc(w_eff_ready, 1)

            v.nop().then_inc(o_added, 1)

            def step(it):
                for slot in range(TILES):
                    at = item(it, slot, LEAD_LOW)
                    if at:
                        g, tile = at
                        u, t = unit_of(tile)
                        dve.wait_ge(t_hi_ready, TILES * g + tile + 1)
                        v.tensor_tensor(pt_lo[:, u % 2, :, t * P:(t + 1) * P],
                                        t_bank[tile % 2][:, :].rearrange("p (j q) -> p j q", q=P),
                                        pt_hi[:, u % 2, :, t * P:(t + 1) * P].bitcast(fp32),
                                        ALU.subtract).then_inc(t_lo_ready, 1)
                    at = item(it, slot, LEAD_EXP)
                    if at:
                        g, tile = at
                        dve.wait_ge(exp_done, TILES * g + tile + 1)
                        v.reciprocal(row_rec[:, tile % 4:tile % 4 + 1],
                                     row_sum[:, tile % 4:tile % 4 + 1]).then_inc(rec_ready, 1)
                    at = item(it, slot, LEAD_S)
                    if at:
                        g, tile = at
                        dve.wait_ge(s_done, TILES * g + tile + 1)
                        v.reduce_max(neg_max[:, tile % 4:tile % 4 + 1], s_bank[tile % 2][:, :], AX_X,
                                     negate=True).then_inc(max_ready, 1)
                    if slot in OUT_SLOTS and item(it, slot, 0):
                        m = OUT_SLOTS.index(slot)
                        dve.wait_ge(o_done, 1 + TT * it + m + 1)
                        if m == 0 and isinstance(it, int):
                            dve.wait_ge(acc_zero, 1)
                        v.tensor_tensor(acc[:, m, :], out_bank[:, :], acc[:, m, :], ALU.add).then_inc(o_added, 1)
                    for hl in range(2):
                        at = item(it, slot, LEAD_VO - 3 * hl)
                        if at and at[1] == 0:
                            g, _ = at
                            dve.wait_ge(m_hi_ready, 4 * g + 2 * hl + 2)
                            v.tensor_tensor(m2[0:KVR, hl, :], work_bank[0:KVR, :], m1[0:KVR, hl, :].bitcast(fp32),
                                            ALU.subtract).then_inc(m_lo_ready, 1)
                    at = item(it, slot, LEAD_ABSORB - 1)
                    if at and at[1] == 0:
                        g, _ = at
                        dve.wait_ge(wh_done, g + 1)
                        v.tensor_tensor(wh[QRB:P, :, 1, :], w_f[QRB:P, :, 1, :], wh[QRB:P, :, 1, :].bitcast(fp32),
                                        ALU.subtract).then_inc(wb_ready, 1)
                    at = item(it, slot, LEAD_Q)
                    if at and at[1] % QT == 0:
                        g, tile = at
                        n = UNITS * g + tile // QT
                        dve.wait_ge(q_raw_ready, n + 1)
                        wait_count(dve, q_hi_ready, n)
                        wait_count(dve, q_lo_ready, n)
                        v.tensor_tensor(q_f[:, :], work_bank[:, :], ropeq[:, 0, :], ALU.mult).then_inc(q_cos_ready, 1)
                    at = item(it, slot, LEAD_PV)
                    if at and at[1] % QT == QT - 1:
                        g, tile = at
                        u, _ = unit_of(tile)
                        n = UNITS * g + u
                        dve.wait_ge(x_hi_ready, 2 * n + 2)
                        v.tensor_tensor(x2[KVR:P, u, :], pv_bank[u % 2][0:KVR, :], x1[0:KVR, u, :].bitcast(fp32),
                                        ALU.subtract).then_inc(x_lo_ready, 1)

            run_steps(dve, step)

            dve.wait_ge(o_added, 1 + TT * PAIRS)
            dve.wait_ge(gates_ready, 2 * B)
            for b in range(B):
                for tt in range(QT * b, QT * b + QT):
                    last = v.tensor_tensor(acc[:, tt, :], acc[:, tt, :], gates[:, 0, b, :], ALU.mult)
                link(last)
                for tt in range(QT * b, QT * b + QT):
                    last = v.tensor_tensor(xs[:, tt, :], xs[:, tt, :], acc[:, tt, :], ALU.add)
                link(last)
                layer_norm(b, var2_ready, sd2_ready, xn2_ready)
                for c in range(2):
                    modulate(b, c, ps[c], xt2_done, HC * b + c + 1, 1, ht2_ready)
            for tt in range(TT):
                dve.wait_ge(ffn_done, tt + 1)
                v.tensor_tensor(acc[:, tt, :], ps[4 + tt % 4][:, :], bias_b[:, :], ALU.add).then_inc(y_biased, 1)
                if tt:
                    dve.wait_ge(y_gated, tt)
                    v.tensor_tensor(acc[:, tt - 1, :], acc[:, tt - 1, :], xs[:, tt - 1, :], ALU.add).then_inc(y_ready, 1)
            dve.wait_ge(y_gated, TT)
            v.tensor_tensor(acc[:, TT - 1, :], acc[:, TT - 1, :], xs[:, TT - 1, :], ALU.add).then_inc(y_ready, 1)

        @block.scalar
        def _(act):
            a = nc.scalar

            def modulate(b, c, bank, turned, count, kind, done):
                act.wait_ge(turned, count)
                a.activation(h_t[:, b, c, :], bank[:, :], ACT.Identity, scale=modc[:, 2 * kind, c, b:b + 1],
                             bias=modc[:, 2 * kind + 1, c, b:b + 1]).then_inc(done, 1)

            act.wait_ge(ld_c, 16)
            a.activation(e_col[:, :, :], c_col[:, :, :], ACT.Exp, scale=-1.0).then_inc(e_ready, 1)
            for b in range(B):
                act.wait_ge(var_ready, b + 1)
                a.activation(sd[:, QT * b:QT * b + QT], sd[:, QT * b:QT * b + QT], ACT.Sqrt).then_inc(sd_ready, 1)
            act.wait_ge(modc_ready, 1)
            for b in range(B):
                for c in range(2, HC):
                    modulate(b, c, ps[4 * b + c], xt_done, HC * b + c + 1, 0, ht_ready[b])
            for b in range(B):
                act.wait_ge(tok_copied, b + 1)
                for t in range(QT):
                    tt = QT * b + t
                    a.activation(junk[:, tt, 0:QR], tok[:, tt, 0:QR], ACT.Square, accum_out=ssq[:, tt, 0:1])
                    last = a.activation(junk[:, tt, QR:QR + KVR], tok[:, tt, 2 * P:2 * P + KVR], ACT.Square,
                                        accum_out=ssq[:, tt, 1:2])
                last.then_inc(ssq_ready, 1)
                act.wait_ge(ssq_ready, b + 1)
                tiles = slice(QT * b, QT * b + QT)
                a.activation(nrm[:, tiles, :], ssq[:, tiles, :], ACT.Sqrt).then_inc(nrm_ready, 1)
            for b in range(B):
                act.wait_ge(kq_turned, 3 * b + 1)
                a.activation(kt_hi[:, b, :], ps[QT * b][:, :], ACT.Copy).then_inc(kqt_hi, 1)
                for j, hi in enumerate((qa_hi, qb_hi)):
                    act.wait_ge(kq_turned, 3 * b + 2 + j)
                    a.activation(hi[:, b, :], ps[QT * b + 1 + j][:, :], ACT.Identity,
                                 scale=gq[:, j:j + 1]).then_inc(kqt_hi, 1)
            for kind in range(2):
                for b in range(B):
                    act.wait_ge(gate_done, 2 * kind + b + 1)
                    bank = (ps[0], ps[1], ps[2], ps[7])[2 * kind + b]
                    a.activation(gates[:, kind, b, :], bank[:, :], ACT.Copy).then_inc(gate_copied, 1)
                    a.activation(gate_abs[:, kind, b, :], bank[:, :], ACT.Abs).then_inc(gate_copied, 1)

            def step(it):
                for slot in range(TILES):
                    at = item(it, slot, LEAD_EXP)
                    if at:
                        g, tile = at
                        n = TILES * g + tile
                        r = tile % 4
                        act.wait_ge(max_ready, n + 1)
                        wait_count(act, t_done, n - 3)
                        a.activation(probs[:, r, :], s_bank[tile % 2][:, :], ACT.Exp, bias=neg_max[:, r:r + 1],
                                     accum_out=row_sum[:, r:r + 1]).then_inc(exp_done, 1)
                    at = item(it, slot, LEAD_T)
                    if at:
                        g, tile = at
                        u, t = unit_of(tile)
                        if t == 0:
                            wait_count(act, pv_done, UNITS * g + u - 1)
                        act.wait_ge(t_done, TILES * g + tile + 1)
                        a.activation(pt_hi[:, u % 2, :, t * P:(t + 1) * P],
                                     t_bank[tile % 2][:, :].rearrange("p (j q) -> p j q", q=P),
                                     ACT.Copy).then_inc(t_hi_ready, 1)
                    at = item(it, slot, LEAD_ABSORB)
                    if at and at[1] == 0:
                        g, _ = at
                        act.wait_ge(absorbed, g + 1)
                        wait_count(act, wl_ready, g)
                        wait_count(act, wb_ready, g)
                        a.activation(w_f[:, :, :, 0:KVR],
                                     work_bank[:, 0:4 * KVR].rearrange("p (h a c) -> p h a c", h=2, a=2),
                                     ACT.Copy).then_inc(w_copied, 1)
                    for hl in range(2):
                        at = item(it, slot, LEAD_VO - 3 * hl)
                        if at and at[1] == 0:
                            g, _ = at
                            act.wait_ge(vo_done, 2 * g + hl + 1)
                            wait_count(act, o_done, 1 + TT * g)
                            a.activation(m1[:, hl, :], work_bank[:, :], ACT.Copy).then_inc(m_hi_ready, 1)
                            a.activation(m2[KVR:P, hl, :], work_bank[KVR:P, :], ACT.Copy).then_inc(m_hi_ready, 1)
                    at = item(it, slot, LEAD_Q)
                    if at and at[1] % QT == 0:
                        g, tile = at
                        n = UNITS * g + tile // QT
                        act.wait_ge(q_done, n + 1)
                        wait_count(act, rot_moved, 32 * n)
                        wait_count(act, q_added, n)
                        a.activation(q_raw[KVR:P, :], work_bank[KVR:P, :], ACT.Copy).then_inc(q_raw_ready, 1)
                    at = item(it, slot, LEAD_Q - 3)
                    if at and at[1] % QT == 0:
                        g, tile = at
                        u, _ = unit_of(tile)
                        n = UNITS * g + u
                        act.wait_ge(q_added, n + 1)
                        wait_count(act, s_done, QT * (n - 1))
                        a.activation(q_hi[:, u % 2, :], q_f[:, :], ACT.Copy).then_inc(q_hi_ready, 1)
                    at = item(it, slot, LEAD_PV)
                    if at and at[1] % QT == QT - 1:
                        g, tile = at
                        u, _ = unit_of(tile)
                        n = UNITS * g + u
                        act.wait_ge(pv_done, n + 1)
                        wait_count(act, o_done, 1 + TT * (g - 1) + (QT if u < 2 else TT))
                        a.activation(x1[:, u, :], pv_bank[u % 2][:, :], ACT.Copy).then_inc(x_hi_ready, 1)
                        a.activation(x2[0:KVR, u, :], pv_bank[u % 2][0:KVR, :], ACT.Copy).then_inc(x_hi_ready, 1)

            run_steps(act, step)

            for b in range(B):
                act.wait_ge(var2_ready, b + 1)
                a.activation(sd[:, QT * b:QT * b + QT], sd[:, QT * b:QT * b + QT], ACT.Sqrt).then_inc(sd2_ready, 1)
                for c in range(2, HC):
                    modulate(b, c, ps[c], xt2_done, HC * b + c + 1, 1, ht2_ready)

        @block.gpsimd
        def _(pool):
            gp = nc.gpsimd
            chain = [0]

            def link(ins):
                chain[0] += 1
                ins.then_inc(pool_step, 1)
                pool.wait_ge(pool_step, chain[0])

            link(gp.memset(one[:, :], 1.0))
            gp.memset(q_rot[:, :], 0.0).then_inc(rot_clear, 1)
            for kind in range(2):
                for b in range(B):
                    pool.wait_ge(gate_copied, 2 * (2 * kind + b + 1))
                    gate, mag = gates[:, kind, b, :], gate_abs[:, kind, b, :]
                    gp.tensor_scalar(mag, mag, 0.25, None, ALU.max)
                    link(gp.tensor_scalar(gate, gate, 0.0, None, ALU.is_ge))
                    link(gp.tensor_scalar(gate, gate, 2.0, -1.0, ALU.mult, ALU.add))
                    gp.tensor_tensor(gate, gate, mag, ALU.mult).then_inc(gates_ready, 1)
            pool.wait_ge(xt_done, TT)
            gp.memset(acc[:, :, :], 0.0).then_inc(acc_zero, 1)

            def step(it):
                for slot in range(TILES):
                    at = item(it, slot, LEAD_EXP)
                    if at:
                        g, tile = at
                        r = tile % 4
                        pool.wait_ge(rec_ready, TILES * g + tile + 1)
                        gp.tensor_tensor(probs[:, r, :], probs[:, r, :],
                                         row_rec[:, r:r + 1].broadcast_to((P, S)), ALU.mult).then_inc(normed, 1)
                    at = item(it, slot, LEAD_ABSORB)
                    if at and at[1] == 0:
                        g, _ = at
                        pool.wait_ge(w_copied, g + 1)
                        pool.wait_ge(ld_wq, 48 * (g + 1))
                        wait_count(pool, q_done, UNITS * g)
                        gp.tensor_tensor(wh[:, :, :, :].rearrange("p h a c -> p (h a c)"),
                                         w_f[:, :, :, :].rearrange("p h a c -> p (h a c)"),
                                         one[:, :].broadcast_to((P, 4 * P)), ALU.mult).then_inc(wh_done, 1)
                        pool.wait_ge(wh_done, g + 1)
                        gp.tensor_tensor(wl[:, :, :], w_f[:, :, 0, :], wh[:, :, 0, :].bitcast(fp32),
                                         ALU.subtract).then_inc(wl_ready, 1)
                    at = item(it, slot, LEAD_Q - 2)
                    if at and at[1] % QT == 0:
                        g, tile = at
                        n = UNITS * g + tile // QT
                        pool.wait_ge(rot_moved, 32 * (n + 1))
                        gp.tensor_tensor(q_rot[:, :], q_rot[:, :], ropeq[:, 1, :],
                                         ALU.mult).then_inc(q_rotated, 1)
                        pool.wait_ge(q_rotated, n + 1)
                        pool.wait_ge(q_cos_ready, n + 1)
                        gp.tensor_tensor(q_f[:, :], q_f[:, :], q_rot[:, :],
                                         ALU.add).then_inc(q_added, 1)
                    at = item(it, slot, LEAD_Q - 3)
                    if at and at[1] % QT == 0:
                        g, tile = at
                        u, _ = unit_of(tile)
                        n = UNITS * g + u
                        pool.wait_ge(q_hi_ready, n + 1)
                        gp.tensor_tensor(q_lo[:, u % 2, :], q_f[:, :], q_hi[:, u % 2, :].bitcast(fp32),
                                         ALU.subtract).then_inc(q_lo_ready, 1)

            run_steps(pool, step)
            for tt in range(TT):
                pool.wait_ge(y_biased, tt + 1)
                gp.tensor_tensor(acc[:, tt, :], acc[:, tt, :], gates[:, 1, tt // QT, :], ALU.mult).then_inc(y_gated, 1)


def rope_tables():
    exponent = np.arange(0, RD, 2, dtype=np.float32) / np.float32(RD)
    inv_freq = np.float32(1.0) / np.power(10000.0, exponent.astype(np.float64)).astype(np.float32)
    angle = np.outer(np.arange(S, dtype=np.float32), inv_freq).astype(np.float32).astype(np.float64)
    cos = np.concatenate([np.cos(angle)] * 2, -1)
    sin = np.concatenate([-np.sin(angle), np.sin(angle)], -1)
    on_q = np.zeros((P, 2, S), np.float64)
    on_q[:KVR, 0] = SCALING
    on_q[KVR:, 0], on_q[KVR:, 1] = cos.T * SCALING, sin.T * SCALING
    on_k = np.stack([cos, sin]).reshape(2, QT, P, RD).transpose(2, 0, 1, 3)
    return on_q.astype(np.float32), np.ascontiguousarray(on_k.astype(np.float32))


def kernel(**inputs):
    import concourse.bacc as bacc
    from concourse.bass_utils import run_bass_kernel_spmd as run

    a = {name[3:]: np.asarray(value) for name, value in inputs.items()}
    w_qa = a["attn_w_qa"]
    w_qb = a["attn_w_qb"].reshape(QR, NH, ND + RD)
    w_kvb = a["attn_w_kvb"].reshape(KVR, NH, ND + VD)
    rows = np.r_[0:QR, P:QR]
    nope_t = w_qb[rows, :, :ND].transpose(1, 2, 0)
    w_k_t = w_kvb[:, :, :ND].transpose(1, 2, 0)
    w_v_t = w_kvb[:, :, ND:].transpose(1, 2, 0)
    rope = w_qb[rows, :, ND:].reshape(2, P, NH, RD).transpose(2, 1, 0, 3)
    w_o = a["attn_w_o"].reshape(NH, VD, H)

    def pairs(t):
        return t.reshape(PAIRS, 2, *t.shape[1:]).swapaxes(1, 2)

    rope_q, rope_k = rope_tables()
    g_qa = a["attn_g_qa"]
    arrays = {
        "x": a["attn_hidden_states"],
        "w_lat": np.concatenate([w_qa, w_qa[:, P:], a["attn_w_kva"]], 1),
        "g_lat_q": np.stack([g_qa[:P], np.tile(g_qa[P:], 2)], 1),
        "g_lat_k": a["attn_g_kva"],
        "wq_pack": pairs(np.concatenate([nope_t, w_k_t], -1)),
        "rope_pack": pairs(rope),
        "wo_pack": pairs(np.concatenate([w_v_t, w_v_t, w_o], -1)),
        "lora_a": a["ffn_lora_A"].reshape(P, H),
        "lora_b": a["ffn_lora_B"].transpose(0, 2, 1).reshape(P, H),
        "lora_w": np.repeat(a["ffn_lora_weights"], P // a["ffn_lora_weights"].shape[0])[:, None],
        "w_ffn_t": a["ffn_W"].T,
        "bias": a["ffn_bias"],
        "c_t": a["c"].T,
        "w_mod": a["wmod"],
        "ident_in": np.eye(P, dtype=np.float32),
        "rope_q": rope_q,
        "rope_k": rope_k,
    }
    arrays = {f"in_{name}": np.ascontiguousarray(value) for name, value in arrays.items()}
    nc = bacc.Bacc("TRN2", target_bir_lowering=False, num_devices=1)
    args = [nc.dram_tensor(name, value.shape, mybir.dt.from_np(value.dtype), kind="ExternalInput").ap()
            for name, value in arrays.items()]
    out = nc.dram_tensor("out", (B, S, H), mybir.dt.float32, kind="ExternalOutput").ap()
    build(nc, *args, out)
    return run(nc, [arrays], core_ids=[0]).results[0]["out"]
```

```python
from contextlib import ExitStack

import numpy as np

import concourse.bass as bass
from concourse import mybir

B, S, H = 2, 512, 512
NH = 32
QR, KVR, RD, ND, VD = 192, 64, 64, 128, 128
P = 128
QT = S // P
TT = B * QT
HC = H // P
QRB = QR - P
PAIRS = NH // 2
UNITS = 2 * B
TILES = UNITS * QT
LP = QR + KVR + RD
LW = LP + QRB
WQ_COLS = 2 * P + KVR
WO_COLS = P + H
SCALING = (ND + RD) ** -0.5
EPS_LN, EPS_RMS = 1e-5, 1e-6
SHIFT_A, SCALE_A, GATE_A, SHIFT_B, SCALE_B, GATE_B = range(6)

LEAD_LOAD_WQ = 36
LEAD_ABSORB = 29
LEAD_SPLIT = 29
LEAD_Q = 24
LEAD_Q_RAW = 23
LEAD_Q_COS = 22
LEAD_ROPE = 22
LEAD_Q_HI = 21
LEAD_Q_LO = 20
LEAD_S = 18
LEAD_EXP = 17
LEAD_NORM = 16
LEAD_T = 15
LEAD_LOW = 14
LEAD_LOAD_WO = 13
LEAD_PV = 11
LEAD_X = 10
LEAD_X_HI = 9
LEAD_X_LO = 8
LEAD_VO = 1
OUT_SLOTS = (5, 6, 7, 9, 10, 11, 13, 14)
LORA_SLOTS = (8, 10, 12, 14)
RAMP = 3


def build(nc, x, w_lat, g_lat_q, g_lat_k, wq_pack, rope_pack, wo_pack, lora_a, lora_b, lora_w,
          w_ffn_t, bias, c_t, w_mod, ident_in, rope_q, rope_k, out):
    fp32 = mybir.dt.float32
    f32r = mybir.dt.float32r
    ALU = mybir.AluOpType
    ACT = mybir.ActivationFunctionType
    AX_X = mybir.AxisListType.X

    x_v = x.rearrange("b (t p) d -> p b t d", p=P)
    out_v = out.rearrange("b (t p) d -> p (b t) d", p=P)
    w_mod_v = w_mod.rearrange("(c p) (s n) -> s p c n", p=P, s=6)

    ctx = ExitStack()
    with ctx:
        def sb(name, shape, dt=fp32, where=ctx):
            return where.enter_context(nc.sbuf_tensor(name, shape, dt))

        def sem(name):
            return ctx.enter_context(nc.semaphore(name))

        xs = sb("xs", [P, TT, H])
        acc = sb("acc", [P, TT, H])
        h_t = sb("h_t", [P, B, HC, S])
        ident = sb("ident", [P, P])
        ropeq = sb("ropeq", [P, 2, S])
        ropek = sb("ropek", [P, 2, QT, RD])
        gq = sb("gq", [P, 2])
        gk = sb("gk", [P, KVR])
        gates = sb("gates", [P, 2, B, H])
        modc = sb("modc", [P, 4, HC, B])
        stats = sb("stats", [P, TT, 6])
        mv = sb("mv", [P, TT, 2])
        sd = sb("sd", [P, TT])
        rs = sb("rs", [P, TT])
        w_eff = sb("w_eff", [P, HC, H])
        bias_b = sb("bias_b", [P, H])
        kt_hi = sb("kt_hi", [P, B, S], f32r)
        kt_lo = sb("kt_lo", [P, B, S], f32r)
        kc = sb("kc", [P, B, QT, P], f32r)
        qa_hi = sb("qa_hi", [P, B, S], f32r)
        qa_lo = sb("qa_lo", [P, B, S], f32r)
        qb_hi = sb("qb_hi", [P, B, S], f32r)
        qb_lo = sb("qb_lo", [P, B, S], f32r)

        first = ExitStack()
        w_l = sb("w_l", [P, HC, LP], where=first)
        tok = sb("tok", [P, TT, LW], where=first)
        kp = sb("kp", [P, TT, P], where=first)
        c_col = sb("c_col", [P, HC, B], where=first)
        e_col = sb("e_col", [P, HC, B], where=first)
        spare = 3 * QT * S - (HC * LP + TT * LW + TT * P + 2 * HC * B)
        sb("spare", [P, spare], where=first)
        wm = sb("wm", [P, 4, HC, H], where=first)
        first.close()
        wm_gate = sb("wm_gate", [P, HC, H], where=first)
        first.close()

        pt_hi = sb("pt_hi", [P, 2, QT, S], f32r)
        pt_lo = sb("pt_lo", [P, 2, QT, S], f32r)
        x_low = sb("x_low", [P, B, S])
        x_f = sb("x_f", [P, B, S])
        x_hi = sb("x_hi", [P, B, S], f32r)
        x_lo = sb("x_lo", [P, B, S], f32r)
        m_hi = sb("m_hi", [P, H], f32r)
        m_lo = sb("m_lo", [P, H], f32r)
        wo_in = sb("wo_in", [P, 2, WO_COLS])
        probs = sb("probs", [P, 4, S])
        q_raw = sb("q_raw", [P, S])
        q_rot = sb("q_rot", [P, S])
        q_f = sb("q_f", [P, S])
        q_hi = sb("q_hi", [P, 2, S], f32r)
        q_lo = sb("q_lo", [P, 2, S], f32r)
        wq_in = sb("wq_in", [P, 2, WQ_COLS])
        w_f = sb("w_f", [P, 2, 2, P])
        wh = sb("wh", [P, 2, 2, P], f32r)
        wl = sb("wl", [P, 2, P], f32r)
        s_col = sb("s_col", [P, HC, B])
        s_bc = sb("s_bc", [P, HC, B, P])
        one = sb("one", [P, 1])
        neg_max = sb("neg_max", [P, 4])
        row_sum = sb("row_sum", [P, 4])
        row_rec = sb("row_rec", [P, 4])
        gate_abs = sb("gate_abs", [P, 2, B, H])
        lora_a_sb = sb("lora_a_sb", [P, H])
        lora_b_sb = sb("lora_b_sb", [P, H])
        lora_w_sb = sb("lora_w_sb", [P, 1])
        ssq = sb("ssq", [P, TT, 2])
        nrm = sb("nrm", [P, TT, 2])
        gate_bias = gate_abs[:, 0]
        junk = gate_abs[:, :, :, :].rearrange("p k b (h n) -> p (k b h) n", h=2)
        k_rot = sb("k_rot", [P, QT, RD])

        ps = [ctx.enter_context(nc.psum_tensor(f"ps{i}", [P, S], fp32)) for i in range(8)]
        s_bank, t_bank = ps[0:2], ps[2:4]
        pv_bank = ps[4:6]
        out_bank = ps[6]
        q_bank = ps[7]

        ld_x = [sem(f"ld_x{b}") for b in range(B)]
        ld_ident, ld_c, ld_wl, ld_small, ld_lora = (sem(n) for n in ("ld_ident", "ld_c", "ld_wl", "ld_small", "ld_lora"))
        ld_mod = [sem(f"ld_mod{i}") for i in range(6)]
        ld_wq, ld_wo, rot_moved, stored = (sem(n) for n in ("ld_wq", "ld_wo", "rot_moved", "stored"))
        ve, pool_step = sem("ve"), sem("pool_step")
        var_ready, sd_ready, xn_ready, xt_done = (sem(n) for n in ("var_ready", "sd_ready", "xn_ready", "xt_done"))
        e_ready, silu_ready, silu_bc, modc_done, modc_ready = (
            sem(n) for n in ("e_ready", "silu_ready", "silu_bc", "modc_done", "modc_ready"))
        mod_used = [sem(f"mod_used{i}") for i in range(2)]
        mod2_done = sem("mod2_done")
        ht_ready = [sem(f"ht_ready{b}") for b in range(B)]
        tok_done, tok_copied, ssq_ready, nrm_ready = (sem(n) for n in ("tok_done", "tok_copied", "ssq_ready", "nrm_ready"))
        kq_ready, kq_turned, kqt_hi, kqt_lo, kc_ready = (sem(n) for n in ("kq_ready", "kq_turned", "kqt_hi", "kqt_lo", "kc_ready"))
        gate_done, gate_copied, att_gates_ready, ffn_gates_ready, lora_b_ready, lora_done, w_eff_ready = (
            sem(n) for n in ("gate_done", "gate_copied", "att_gates_ready", "ffn_gates_ready", "lora_b_ready", "lora_done", "w_eff_ready"))
        acc_zero, att_gated, res_ready, xb_ready, ffn_done, y_gated, y_ready = (
            sem(n) for n in ("acc_zero", "att_gated", "res_ready", "xb_ready", "ffn_done", "y_gated", "y_ready"))
        xn2_ready, xt2_done, ht2_first, ht2_second, var2_ready, sd2_ready, rs2_ready = (
            sem(n) for n in ("xn2_ready", "xt2_done", "ht2_first", "ht2_second", "var2_ready", "sd2_ready",
                             "rs2_ready"))
        absorbed, w_copied, wh_done, wl_ready, wb_ready, rot_clear = (
            sem(n) for n in ("absorbed", "w_copied", "wh_done", "wl_ready", "wb_ready", "rot_clear"))
        q_done, q_raw_ready, q_cos_ready, q_rotated, q_added, q_hi_ready, q_lo_ready = (
            sem(n) for n in ("q_done", "q_raw_ready", "q_cos_ready", "q_rotated", "q_added", "q_hi_ready", "q_lo_ready"))
        s_done, max_ready, exp_done, rec_ready, normed, normed_act = (
            sem(n) for n in ("s_done", "max_ready", "exp_done", "rec_ready", "normed", "normed_act"))
        t_done, t_hi_ready, t_lo_ready, pv_done, x_low_ready, x_ready, x_hi_ready, x_lo_ready = (
            sem(n) for n in ("t_done", "t_hi_ready", "t_lo_ready", "pv_done", "x_low_ready", "x_ready", "x_hi_ready",
                             "x_lo_ready"))
        vo_done, m_hi_ready, m_lo_ready, o_done, o_added = (
            sem(n) for n in ("vo_done", "m_hi_ready", "m_lo_ready", "o_done", "o_added"))

        block = ctx.enter_context(nc.Block())

        def item(it, slot, lead, per_step=TILES):
            ahead, local = divmod(slot + lead, per_step)
            step = it + ahead
            if isinstance(step, int) and not 0 <= step < PAIRS:
                return None
            return step, local

        def is_first(at):
            return isinstance(at[0], int) and at[0] == 0

        def wait_count(eng, semaphore, count):
            if not isinstance(count, int) or count > 0:
                eng.wait_ge(semaphore, count)

        def run_steps(eng, step):
            for it in range(-RAMP, 0):
                step(it)
            with eng.Fori(0, PAIRS - RAMP) as it:
                step(it)
            for it in range(PAIRS - RAMP, PAIRS):
                step(it)

        def finish_gate(engine, link, kind):
            gate, mag = (t[:, kind, :, :].rearrange("p b n -> p (b n)") for t in (gates, gate_abs))
            engine.tensor_scalar(mag, mag, 0.25, None, ALU.max)
            link(engine.tensor_scalar(gate, gate, 0.0, None, ALU.is_ge))
            link(engine.tensor_scalar(gate, gate, 2.0, -1.0, ALU.mult, ALU.add))
            return engine.tensor_tensor(gate, gate, mag, ALU.mult)

        def last_out_bank(tt):
            return (ps[6], ps[0])[tt % 2]

        def turn_banks(tt):
            return (ps[1:3], ps[4:6])[tt % 2]

        def ffn_bank(tt):
            return (ps[3], ps[7])[tt % 2]

        def gate_bank(i):
            return (ps[4], ps[5], ps[3], ps[7])[i]

        def unit_of(tile):
            return tile // QT, tile % QT

        def head_batch(u):
            return divmod(u, B)

        def half(hl):
            return slice(hl * KVR, (hl + 1) * KVR)

        def on_scalar(tile):
            return tile % QT == QT - 1

        def normed_by(tile, g):
            before = sum(on_scalar(k) == on_scalar(tile) for k in range(tile + 1))
            each = TILES // QT if on_scalar(tile) else TILES - TILES // QT
            return (normed_act if on_scalar(tile) else normed), each * g + before

        @block.sync
        def _(sp):
            def load_wq(g):
                sp.dma_start(wq_in[:, :, :], wq_pack[g]).then_inc(ld_wq, 16)
                for ab in range(2):
                    sp.dma_start(w_f[:, :, ab, KVR:P], rope_pack[g][:, :, ab]).then_inc(ld_wq, 16)

            sp.dma_start(c_col[:, :, :], c_t.rearrange("(c p) b -> p c b", p=P)).then_inc(ld_c, 16)
            sp.dma_start(ident[:, :], ident_in).then_inc(ld_ident, 16)
            sp.dma_start(xs[:, 0:QT, :], x_v[:, 0]).then_inc(ld_x[0], 16)
            sp.dma_start(wm[:, 0], w_mod_v[SCALE_A]).then_inc(ld_mod[SCALE_A], 16)
            sp.dma_start(wm[:, 1], w_mod_v[SHIFT_A]).then_inc(ld_mod[SHIFT_A], 16)
            sp.dma_start(w_l[:, :, :], w_lat.rearrange("(c p) n -> p c n", p=P)).then_inc(ld_wl, 16)
            sp.dma_start(xs[:, QT:TT, :], x_v[:, 1]).then_inc(ld_x[1], 16)
            load_wq(0)
            sp.dma_start(ropek[:, :, :, :], rope_k).then_inc(ld_small, 16)
            sp.dma_start(ropeq[:, :, :], rope_q).then_inc(ld_small, 16)
            sp.dma_start(gq[:, :], g_lat_q).then_inc(ld_small, 16)
            sp.dma_start(gk[:, :], g_lat_k.partition_broadcast(P)).then_inc(ld_small, 16)
            sp.dma_start(bias_b[:, :], bias.partition_broadcast(P)).then_inc(ld_small, 16)
            sp.dma_start(wm[:, 3], w_mod_v[GATE_A]).then_inc(ld_mod[GATE_A], 16)
            sp.wait_ge(mod_used[0], 1)
            sp.dma_start(wm[:, 0], w_mod_v[SHIFT_B]).then_inc(ld_mod[SHIFT_B], 16)
            sp.dma_start(wm[:, 2], w_mod_v[SCALE_B]).then_inc(ld_mod[SCALE_B], 16)
            sp.dma_start(lora_a_sb[:, :], lora_a).then_inc(ld_lora, 16)
            sp.dma_start(lora_b_sb[:, :], lora_b).then_inc(ld_lora, 16)
            sp.dma_start(lora_w_sb[:, :], lora_w).then_inc(ld_lora, 16)
            sp.dma_start(w_eff[:, :, :], w_ffn_t.rearrange("(c p) n -> p c n", p=P)).then_inc(ld_lora, 16)

            def step(it):
                for slot in range(TILES):
                    at = item(it, slot, LEAD_LOAD_WQ)
                    if at and at[1] == 0 and not is_first(at):
                        g, _ = at
                        wait_count(sp, wl_ready, 2 * g)
                        wait_count(sp, wb_ready, 2 * g)
                        load_wq(g)
                    at = item(it, slot, LEAD_LOAD_WO)
                    if at and at[1] == 0:
                        g, _ = at
                        wait_count(sp, vo_done, g)
                        if is_first(at):
                            sp.wait_ge(gate_done, B)
                        sp.dma_start(wo_in[:, :, :], wo_pack[g]).then_inc(ld_wo, 16)
                    at = item(it, slot, LEAD_Q_RAW)
                    if at and at[1] % QT == 0:
                        g, tile = at
                        n = UNITS * g + tile // QT
                        sp.wait_ge(q_raw_ready, n + 1)
                        sp.dma_start(q_rot[64:96, :], q_raw[96:128, :]).then_inc(rot_moved, 16)
                        sp.dma_start(q_rot[96:128, :], q_raw[64:96, :]).then_inc(rot_moved, 16)

            sp.wait_ge(rot_clear, 1)
            run_steps(sp, step)
            sp.wait_ge(pv_done, UNITS * PAIRS - 1)
            sp.dma_start(wm_gate[:, :, :], w_mod_v[GATE_B]).then_inc(ld_mod[GATE_B], 16)
            for tt in range(TT):
                sp.wait_ge(y_ready, tt + 1)
                sp.dma_start(out_v[:, tt, :], acc[:, tt, :]).then_inc(stored, 16)
            sp.wait_ge(stored, 16 * TT)

        @block.tensor
        def _(pe):
            mm = nc.tensor.matmul

            def turn_x(b, ready, count, done, banks):
                pe.wait_ge(ready, count)
                for c in range(HC):
                    for t in range(QT):
                        last = nc.tensor.transpose(banks[c][:, t * P:(t + 1) * P],
                                                   acc[:, QT * b + t, c * P:(c + 1) * P], ident[:, :])
                    last.then_inc(done, 1)

            def mod_columns(bank, place, buf, section, done, chunks=range(HC)):
                pe.wait_ge(ld_mod[section], 16)
                for n in chunks:
                    col = (place * HC + n) * B
                    for k in range(HC):
                        last = mm(bank[:, col:col + B], wm[:, buf, k, n * P:(n + 1) * P], s_col[:, k, :],
                                  start=(k == 0), stop=(k == HC - 1))
                last.then_inc(done, 1)

            def absorb():
                for hl in range(2):
                    for ab in range(2):
                        col = (2 * hl + ab) * KVR
                        last = mm(q_bank[:, col:col + KVR], wq_in[:, hl, ab * P:(ab + 1) * P],
                                  wq_in[:, hl, 2 * P:WQ_COLS], start=True, stop=True)
                last.then_inc(absorbed, 1)

            def turn_latents(b):
                pe.wait_ge(kq_ready, b + 1)
                for j in range(3):
                    for t in range(QT):
                        tt = QT * b + t
                        src = kp[:, tt, :] if j == 0 else tok[:, tt, (j - 1) * P:j * P]
                        last = nc.tensor.transpose(ps[j][:, t * P:(t + 1) * P], src, ident[:, :])
                    last.then_inc(kq_turned, 1)

            pe.wait_ge(silu_ready, 1)
            mod_columns(ps[7], 0, 0, SCALE_A, mod_used[0])
            pe.wait_ge(ld_ident, 16)
            turn_x(0, xn_ready, QT, xt_done, ps[0:4])
            mod_columns(ps[7], 1, 1, SHIFT_A, mod_used[1])
            pe.wait_ge(modc_ready, 1)
            turn_x(1, xn_ready, TT, xt_done, ps[4:8])
            pe.wait_ge(ld_wl, 16)
            for b in range(B):
                pe.wait_ge(ht_ready[b], HC)
                if b:
                    pe.wait_ge(ld_wq, 48)
                    absorb()
                for t in range(QT):
                    tt = QT * b + t
                    if tt == TT - 1:
                        pe.wait_ge(w_copied, 1)
                    for c in range(HC):
                        last = mm(ps[tt][:, 0:LP], h_t[:, b, c, t * P:(t + 1) * P], w_l[:, c, :],
                                  start=(c == 0), stop=(c == HC - 1))
                    last.then_inc(tok_done, 1)
            turn_latents(0)
            pe.wait_ge(tok_copied, B)
            pe.wait_ge(kqt_lo, 3)
            pe.nop().then_inc(o_done, TT)

            def project(it, m, bank):
                b, t = divmod(m, QT)
                if m == 0:
                    pe.wait_ge(m_lo_ready, it + 1)
                if t == 0:
                    pe.wait_ge(x_hi_ready, B * it + b + 1)
                    pe.wait_ge(x_lo_ready, B * it + b + 1)
                cols = slice(t * P, (t + 1) * P)
                mm(bank[:, :], x_lo[:, b, cols], m_hi[:, :], start=True, stop=False)
                mm(bank[:, :], x_hi[:, b, cols], m_lo[:, :], start=False, stop=False)
                mm(bank[:, :], x_hi[:, b, cols], m_hi[:, :], start=False, stop=True).then_inc(o_done, 1)

            def gate_half(i, weights, odd):
                for k in range(odd * HC // 2, (odd + 1) * HC // 2):
                    last = mm(gate_bank(i)[:, :], s_bc[:, k, i % B, :], weights[:, k, :],
                              start=(k == 0), stop=(k == HC - 1))
                if odd:
                    last.then_inc(gate_done, 1)

            def ramp_work(it, slot):
                if it == -2 and slot == 11:
                    turn_latents(1)
                if it == -2 and slot == 12:
                    pe.wait_ge(kqt_lo, 6)
                    pe.wait_ge(kc_ready, B)
                if it == -2 and 8 <= slot < 12:
                    b, odd = divmod(slot - 8, 2)
                    if slot == 8:
                        pe.wait_ge(ld_mod[GATE_A], 16)
                        pe.wait_ge(silu_bc, 1)
                    gate_half(b, wm[:, 3], odd)
                piece = TILES * (it + 1) + slot + 2
                if 0 <= piece < 2 * HC:
                    place, n = divmod(piece, HC)
                    place = 1 - place
                    mod_columns(out_bank, place, (2, 0)[place], (SCALE_B, SHIFT_B)[place], mod2_done, (n,))
                if it == -1 and slot in LORA_SLOTS:
                    c = LORA_SLOTS.index(slot)
                    if c == 0:
                        pe.wait_ge(lora_b_ready, 1)
                        pe.wait_ge(modc_ready, 2)
                    else:
                        pe.wait_ge(w_eff_ready, c)
                    mm(out_bank[:, :], lora_a_sb[:, c * P:(c + 1) * P], lora_b_sb[:, :],
                       start=True, stop=True).then_inc(lora_done, 1)

            def step(it):
                for slot in range(TILES):
                    if isinstance(it, int):
                        ramp_work(it, slot)
                    at = item(it, slot, LEAD_T)
                    if at:
                        g, tile = at
                        n = TILES * g + tile
                        pe.wait_ge(*normed_by(tile, g))
                        wait_count(pe, t_hi_ready, n - 1)
                        wait_count(pe, t_lo_ready, n - 1)
                        for j in range(QT):
                            last = nc.tensor.transpose(t_bank[tile % 2][:, j * P:(j + 1) * P],
                                                       probs[:, tile % 4, j * P:(j + 1) * P], ident[:, :])
                        last.then_inc(t_done, 1)

                    at = item(it, slot, LEAD_S)
                    if at:
                        g, tile = at
                        n = TILES * g + tile
                        u, t = unit_of(tile)
                        if t == 0:
                            pe.wait_ge(q_hi_ready, UNITS * g + u + 1)
                            pe.wait_ge(q_lo_ready, UNITS * g + u + 1)
                        wait_count(pe, exp_done, n - 1)
                        bank, cols, b = s_bank[tile % 2], slice(t * P, (t + 1) * P), head_batch(u)[1]
                        mm(bank[:, :], q_lo[:, u % 2, cols], kt_hi[:, b, :], start=True, stop=False)
                        mm(bank[:, :], q_hi[:, u % 2, cols], kt_lo[:, b, :], start=False, stop=False)
                        mm(bank[:, :], q_hi[:, u % 2, cols], kt_hi[:, b, :], start=False,
                           stop=True).then_inc(s_done, 1)

                    at = item(it, slot, LEAD_ABSORB)
                    if at and at[1] == 0 and not is_first(at):
                        g, _ = at
                        pe.wait_ge(ld_wq, 48 * (g + 1))
                        wait_count(pe, q_cos_ready, UNITS * (g - 1) + UNITS - 1)
                        absorb()

                    at = item(it, slot, LEAD_Q)
                    if at and at[1] % QT == 0:
                        g, tile = at
                        u, _ = unit_of(tile)
                        n = UNITS * g + u
                        hl, b = head_batch(u)
                        if b == 0:
                            pe.wait_ge(wl_ready, 2 * g + hl + 1)
                            pe.wait_ge(wb_ready, 2 * g + hl + 1)
                        if u == UNITS - 1:
                            pe.wait_ge(w_copied, min(g + 2, PAIRS) if isinstance(g, int) else g + 2)
                        else:
                            wait_count(pe, q_cos_ready, n)
                        mm(q_bank[:, :], wl[:, hl, :], qa_hi[:, b, :], start=True, stop=False)
                        mm(q_bank[:, :], wh[:, hl, 0, :], qa_lo[:, b, :], start=False, stop=False)
                        mm(q_bank[:, :], wh[0:QRB, hl, 1, :], qb_lo[0:QRB, b, :], start=False, stop=False)
                        mm(q_bank[:, :], wh[:, hl, 1, :], qb_hi[:, b, :], start=False, stop=False)
                        mm(q_bank[:, :], wh[:, hl, 0, :], qa_hi[:, b, :], start=False,
                           stop=True).then_inc(q_done, 1)

                    at = item(it, slot, LEAD_PV)
                    if at:
                        g, tile = at
                        u, t = unit_of(tile)
                        n = UNITS * g + u
                        if t == 0:
                            pe.wait_ge(t_hi_ready, QT * n + QT)
                            wait_count(pe, x_ready, n - 1)
                        if t == QT // 2:
                            pe.wait_ge(t_lo_ready, QT * n + QT)
                        part = pt_hi if t < QT // 2 else pt_lo
                        for j in (2 * t % QT, 2 * t % QT + 1):
                            last = mm(pv_bank[u % 2][:, :], kc[:, head_batch(u)[1], j, :], part[:, u % 2, j, :],
                                      start=(t == 0 and j == 0), stop=(t == QT - 1 and j == QT - 1))
                        if t == QT - 1:
                            last.then_inc(pv_done, 1)

                    if slot in OUT_SLOTS and item(it, slot, 0) and not (isinstance(it, int) and it == PAIRS - 1):
                        m = OUT_SLOTS.index(slot)
                        if m:
                            pe.wait_ge(o_added, TT + TT * it + m)
                        project(it, m, out_bank)

                    for hl in range(2):
                        at = item(it, slot, LEAD_VO - 2 * hl)
                        if at and at[1] == 0:
                            g, _ = at
                            if hl == 0:
                                pe.wait_ge(ld_wo, 16 * (g + 1))
                                pe.wait_ge(o_added, TT + TT * g)
                                if is_first(at):
                                    pe.wait_ge(w_eff_ready, HC)
                            last = mm(out_bank[:, :], wo_in[:, hl, 0:P], wo_in[:, hl, P:WO_COLS],
                                      start=(hl == 0), stop=(hl == 1))
                            if hl == 1:
                                last.then_inc(vo_done, 1)

            run_steps(pe, step)

            for k in range(TT + 4):
                if k < TT:
                    if k >= 2:
                        pe.wait_ge(o_added, TT + TT * (PAIRS - 1) + k - 1)
                    project(PAIRS - 1, k, last_out_bank(k))
                if k == 1:
                    pe.wait_ge(ld_mod[GATE_B], 16)
                    for odd in range(2):
                        gate_half(B, wm_gate, odd)
                if 0 <= k - 3 < TT:
                    tt = k - 3
                    pe.wait_ge(xn2_ready, tt + 1)
                    if tt >= 2:
                        pe.wait_ge(ht2_first, HC // 2 * (tt - 1))
                        pe.wait_ge(ht2_second, HC // 2 * (tt - 1))
                    for c in range(HC):
                        last = nc.tensor.transpose(turn_banks(tt)[c // 2][:, c % 2 * P:(c % 2 + 1) * P],
                                                   acc[:, tt, c * P:(c + 1) * P], ident[:, :])
                        if c % 2:
                            last.then_inc(xt2_done, 1)
                if k == 3:
                    for odd in range(2):
                        gate_half(B + 1, wm_gate, odd)
                if 0 <= k - 4 < TT:
                    tt = k - 4
                    b, t = divmod(tt, QT)
                    pe.wait_ge(ht2_first, HC // 2 * (tt + 1))
                    pe.wait_ge(ht2_second, HC // 2 * (tt + 1))
                    if tt == 0:
                        pe.wait_ge(w_eff_ready, HC)
                    if tt >= 2:
                        pe.wait_ge(y_gated, tt - 1)
                    else:
                        pe.wait_ge(gate_copied, 2 * (B + tt + 1))
                    for c in range(HC):
                        last = mm(ffn_bank(tt)[:, :], h_t[:, b, c, t * P:(t + 1) * P], w_eff[:, c, :],
                                  start=(c == 0), stop=(c == HC - 1))
                    last.then_inc(ffn_done, 1)

        @block.vector
        def _(dve):
            v = nc.vector
            chain = [0]

            def link(ins):
                chain[0] += 1
                ins.then_inc(ve, 1)
                dve.wait_ge(ve, chain[0])

            def layer_norm(b, var_done, sd_done, xn_done):
                tiles = range(QT * b, QT * b + QT)
                for tt in tiles:
                    last = v.bn_stats(stats[:, tt, :], xs[:, tt, :])
                link(last)
                for tt in tiles:
                    last = v.bn_aggr(mv[:, tt, :], stats[:, tt, :])
                link(last)
                span = slice(QT * b, QT * b + QT)
                v.tensor_scalar(sd[:, span], mv[:, span, 1], EPS_LN, None, ALU.add).then_inc(var_done, 1)
                dve.wait_ge(sd_done, b + 1)
                link(v.reciprocal(rs[:, span], sd[:, span]))
                for tt in tiles:
                    v.tensor_scalar(acc[:, tt, :], xs[:, tt, :], mv[:, tt, 0:1], rs[:, tt:tt + 1],
                                    ALU.subtract, ALU.mult).then_inc(xn_done, 1)

            def modulate(b, c, bank, turned, count, kind, done):
                dve.wait_ge(turned, count)
                v.tensor_scalar(h_t[:, b, c, :], bank[:, :], modc[:, 2 * kind, c, b:b + 1],
                                modc[:, 2 * kind + 1, c, b:b + 1], ALU.mult, ALU.add).then_inc(done, 1)

            dve.wait_ge(ld_c, 16)
            dve.wait_ge(e_ready, 1)
            link(v.tensor_scalar(s_col[:, :, :], e_col[:, :, :], 1.0, None, ALU.add))
            link(v.reciprocal(e_col[:, :, :], s_col[:, :, :]))
            v.tensor_tensor(s_col[:, :, :], c_col[:, :, :], e_col[:, :, :], ALU.mult).then_inc(silu_ready, 1)
            dve.wait_ge(ld_x[0], 16)
            layer_norm(0, var_ready, sd_ready, xn_ready)
            dve.wait_ge(ld_x[1], 16)
            layer_norm(1, var_ready, sd_ready, xn_ready)
            dve.wait_ge(silu_ready, 1)
            v.tensor_copy(s_bc[:, :, :, :], s_col[:, :, :].unsqueeze(3).broadcast_to((P, HC, B, P))).then_inc(silu_bc, 1)
            dve.wait_ge(mod_used[1], 1)
            v.tensor_scalar(modc[:, 0], ps[7][:, 0:HC * B].rearrange("p (n b) -> p n b", b=B), 1.0, None, ALU.add)
            link(v.tensor_copy(modc[:, 1], ps[7][:, HC * B:2 * HC * B].rearrange("p (n b) -> p n b", b=B)))
            v.nop().then_inc(modc_ready, 1)
            for b in range(B):
                for c in range(2):
                    modulate(b, c, ps[4 * b + c], xt_done, HC * b + c + 1, 0, ht_ready[b])
            dve.wait_ge(ld_small, 16 * 5)

            def copy_tokens(b):
                for t in range(QT):
                    tt = QT * b + t
                    dve.wait_ge(tok_done, tt + 1)
                    v.tensor_copy(tok[:, tt, 0:QR], ps[tt][:, 0:QR])
                    last = v.tensor_copy(tok[:, tt, QR:LW], ps[tt][:, P:LP])
                last.then_inc(tok_copied, 1)

            def latents(b):
                tiles = slice(QT * b, QT * b + QT)
                dve.wait_ge(tok_copied, b + 1)
                kr = tok[:, tiles, 2 * P + KVR:LW]
                v.tensor_tensor(kp[:, tiles, KVR:P], kr, ropek[:, 0], ALU.mult)
                v.tensor_tensor(k_rot[:, :, 0:RD // 2], kr[:, :, RD // 2:RD], ropek[:, 1, :, 0:RD // 2], ALU.mult)
                link(v.tensor_tensor(k_rot[:, :, RD // 2:RD], kr[:, :, 0:RD // 2], ropek[:, 1, :, RD // 2:RD], ALU.mult))
                v.tensor_tensor(kp[:, tiles, KVR:P], kp[:, tiles, KVR:P], k_rot[:, :, :], ALU.add)
                dve.wait_ge(nrm_ready, b + 1)
                v.tensor_scalar(nrm[:, tiles, 0], nrm[:, tiles, 0], QR ** -0.5, EPS_RMS, ALU.mult, ALU.add)
                link(v.tensor_scalar(nrm[:, tiles, 1], nrm[:, tiles, 1], KVR ** -0.5, EPS_RMS, ALU.mult, ALU.add))
                link(v.reciprocal(ssq[:, tiles, :], nrm[:, tiles, :]))
                for tt in range(QT * b, QT * b + QT):
                    v.scalar_tensor_tensor(kp[:, tt, 0:KVR], tok[:, tt, 2 * P:2 * P + KVR], ssq[:, tt, 1:2],
                                           gk[:, :], ALU.mult, ALU.mult)
                for tt in range(QT * b, QT * b + QT):
                    last = v.tensor_scalar(tok[:, tt, 0:2 * P], tok[:, tt, 0:2 * P], ssq[:, tt, 0:1], None, ALU.mult)
                last.then_inc(kq_ready, 1)
                dve.wait_ge(kq_ready, b + 1)
                link(v.tensor_copy(kc[:, b, :, 0:KVR], kp[:, tiles, 0:KVR]))
                v.tensor_tensor(kc[:, b, :, KVR:P], kp[:, tiles, 0:KVR], kc[:, b, :, 0:KVR].bitcast(fp32),
                                ALU.subtract).then_inc(kc_ready, 1)

            def low_parts(b):
                dve.wait_ge(kqt_hi, 3 * b + 1)
                v.tensor_tensor(kt_lo[:, b, :], ps[0][:, :], kt_hi[:, b, :].bitcast(fp32),
                                ALU.subtract).then_inc(kqt_lo, 1)
                for j, (hi, lo) in enumerate(((qa_hi, qa_lo), (qb_hi, qb_lo))):
                    dve.wait_ge(kqt_hi, 3 * b + 2 + j)
                    v.scalar_tensor_tensor(lo[:, b, :], ps[1 + j][:, :], gq[:, j:j + 1],
                                           hi[:, b, :].bitcast(fp32), ALU.mult, ALU.subtract).then_inc(kqt_lo, 1)

            copy_tokens(0)
            latents(0)
            copy_tokens(1)
            low_parts(0)
            dve.wait_ge(ld_lora, 16 * 4)
            v.tensor_scalar(lora_b_sb[:, :], lora_b_sb[:, :], lora_w_sb[:, 0:1], 2.0, ALU.mult,
                            ALU.mult).then_inc(lora_b_ready, 1)

            v.nop().then_inc(o_added, TT)

            def ramp_work(it, slot):
                if it == -2 and slot == 6:
                    latents(1)
                if it == -2 and slot == 11:
                    low_parts(1)
                if it == -2 and slot == 13:
                    dve.wait_ge(gate_copied, 2 * B)
                    finish_gate(v, link, 0).then_inc(att_gates_ready, 1)
                if it == -1 and slot == 6:
                    dve.wait_ge(mod2_done, 2 * HC)
                    v.tensor_scalar(modc[:, 2], out_bank[:, 0:HC * B].rearrange("p (n b) -> p n b", b=B),
                                    1.0, None, ALU.add)
                    link(v.tensor_copy(modc[:, 3], out_bank[:, HC * B:2 * HC * B].rearrange("p (n b) -> p n b", b=B)))
                    v.nop().then_inc(modc_ready, 1)
                if it == -1 and slot - 1 in LORA_SLOTS:
                    c = LORA_SLOTS.index(slot - 1)
                    dve.wait_ge(lora_done, c + 1)
                    v.tensor_tensor(w_eff[:, c, :], out_bank[:, :], w_eff[:, c, :], ALU.add).then_inc(w_eff_ready, 1)

            def step(it):
                for slot in range(TILES):
                    if isinstance(it, int):
                        ramp_work(it, slot)
                    if slot - 1 in OUT_SLOTS and item(it, slot, 0) and not (isinstance(it, int) and it == PAIRS - 1):
                        m = OUT_SLOTS.index(slot - 1)
                        dve.wait_ge(o_done, TT + TT * it + m + 1)
                        if m == 0 and isinstance(it, int):
                            dve.wait_ge(acc_zero, 1)
                        v.tensor_tensor(acc[:, m, :], out_bank[:, :], acc[:, m, :], ALU.add).then_inc(o_added, 1)
                    at = item(it, slot, LEAD_LOW)
                    if at:
                        g, tile = at
                        u, t = unit_of(tile)
                        dve.wait_ge(t_hi_ready, TILES * g + tile + 1)
                        v.tensor_tensor(pt_lo[:, u % 2, :, t * P:(t + 1) * P],
                                        t_bank[tile % 2][:, :].rearrange("p (j q) -> p j q", q=P),
                                        pt_hi[:, u % 2, :, t * P:(t + 1) * P].bitcast(fp32),
                                        ALU.subtract).then_inc(t_lo_ready, 1)
                    at = item(it, slot, LEAD_EXP)
                    if at:
                        g, tile = at
                        dve.wait_ge(exp_done, TILES * g + tile + 1)
                        v.reciprocal(row_rec[:, tile % 4:tile % 4 + 1],
                                     row_sum[:, tile % 4:tile % 4 + 1]).then_inc(rec_ready, 1)
                    at = item(it, slot, LEAD_S)
                    if at:
                        g, tile = at
                        dve.wait_ge(s_done, TILES * g + tile + 1)
                        v.reduce_max(neg_max[:, tile % 4:tile % 4 + 1], s_bank[tile % 2][:, :], AX_X,
                                     negate=True).then_inc(max_ready, 1)
                    at = item(it, slot, LEAD_Q_COS)
                    if at and at[1] % QT == 0:
                        g, tile = at
                        n = UNITS * g + tile // QT
                        dve.wait_ge(q_raw_ready, n + 1)
                        wait_count(dve, q_hi_ready, n)
                        wait_count(dve, q_lo_ready, n)
                        v.tensor_tensor(q_f[:, :], q_bank[:, :], ropeq[:, 0, :], ALU.mult).then_inc(q_cos_ready, 1)
                    at = item(it, slot, LEAD_X)
                    if at and at[1] % QT == QT - 1:
                        g, tile = at
                        u, _ = unit_of(tile)
                        hl, b = head_batch(u)
                        dve.wait_ge(x_low_ready, UNITS * g + u + 1)
                        if hl == 0:
                            wait_count(dve, x_lo_ready, B * (g - 1) + b + 1)
                        v.tensor_tensor(x_f[half(hl), b, :], pv_bank[u % 2][0:KVR, :], x_low[half(hl), b, :],
                                        ALU.add).then_inc(x_ready, 1)
                    at = item(it, slot, LEAD_VO - 4)
                    if at and at[1] == 0:
                        g, _ = at
                        dve.wait_ge(m_hi_ready, g + 1)
                        v.tensor_tensor(m_lo[:, :], out_bank[:, :], m_hi[:, :].bitcast(fp32),
                                        ALU.subtract).then_inc(m_lo_ready, 1)
                    for hl in range(2):
                        at = item(it, slot, LEAD_SPLIT - 1 - 4 * hl)
                        if at and at[1] == 0:
                            g, _ = at
                            dve.wait_ge(wh_done, 2 * g + hl + 1)
                            v.tensor_tensor(wh[QRB:P, hl, 1, :], w_f[QRB:P, hl, 1, :],
                                            wh[QRB:P, hl, 1, :].bitcast(fp32), ALU.subtract).then_inc(wb_ready, 1)

            run_steps(dve, step)

            for k in range(TT + 5):
                if k < TT:
                    tt = k
                    dve.wait_ge(o_done, TT + TT * (PAIRS - 1) + tt + 1)
                    if tt == 0:
                        dve.wait_ge(att_gates_ready, 1)
                    v.tensor_tensor(acc[:, tt, :], last_out_bank(tt)[:, :], acc[:, tt, :], ALU.add).then_inc(o_added, 1)
                    dve.wait_ge(o_added, TT + TT * (PAIRS - 1) + tt + 1)
                    v.tensor_tensor(acc[:, tt, :], acc[:, tt, :], gates[:, 0, tt // QT, :],
                                    ALU.mult).then_inc(att_gated, 1)
                if 0 <= k - 1 < TT:
                    tt = k - 1
                    dve.wait_ge(res_ready, tt + 1)
                    link(v.bn_stats(stats[:, tt, :], xs[:, tt, :]))
                    link(v.bn_aggr(mv[:, tt, :], stats[:, tt, :]))
                    v.tensor_scalar(sd[:, tt:tt + 1], mv[:, tt, 1:2], EPS_LN, None, ALU.add).then_inc(var2_ready, 1)
                if 0 <= k - 3 < TT:
                    tt = k - 3
                    b, t = divmod(tt, QT)
                    dve.wait_ge(xt2_done, 2 * tt + 1)
                    for c in range(HC // 2):
                        v.tensor_scalar(h_t[:, b, c, t * P:(t + 1) * P], turn_banks(tt)[0][:, c * P:(c + 1) * P],
                                        modc[:, 2, c, b:b + 1], modc[:, 3, c, b:b + 1],
                                        ALU.mult, ALU.add).then_inc(ht2_first, 1)
                if 0 <= k - 1 < TT:
                    tt = k - 1
                    dve.wait_ge(sd2_ready, tt + 1)
                    link(v.reciprocal(rs[:, tt:tt + 1], sd[:, tt:tt + 1]))
                    v.scalar_tensor_tensor(sd[:, tt:tt + 1], mv[:, tt, 0:1], -1.0, rs[:, tt:tt + 1],
                                           ALU.mult, ALU.mult).then_inc(rs2_ready, 1)
                if k == 4:
                    dve.wait_ge(gate_copied, 2 * 2 * B)
                    finish_gate(v, link, 1).then_inc(ffn_gates_ready, 1)
                if 0 <= k - 5 < TT:
                    tt = k - 5
                    dve.wait_ge(ffn_done, tt + 1)
                    if tt == 0:
                        dve.wait_ge(ffn_gates_ready, 1)
                    v.tensor_tensor(acc[:, tt, :], ffn_bank(tt)[:, :], gates[:, 1, tt // QT, :],
                                    ALU.mult).then_inc(y_gated, 1)

        @block.scalar
        def _(act):
            a = nc.scalar

            def modulate(b, c, bank, turned, count, kind, done):
                act.wait_ge(turned, count)
                a.activation(h_t[:, b, c, :], bank[:, :], ACT.Identity, scale=modc[:, 2 * kind, c, b:b + 1],
                             bias=modc[:, 2 * kind + 1, c, b:b + 1]).then_inc(done, 1)

            def copy_gate(i):
                act.wait_ge(gate_done, i + 1)
                gate, mag = gates[:, i // B, i % B, :], gate_abs[:, i // B, i % B, :]
                a.activation(gate, gate_bank(i)[:, :], ACT.Copy).then_inc(gate_copied, 1)
                a.activation(mag, gate_bank(i)[:, :], ACT.Abs).then_inc(gate_copied, 1)

            def copy_absorbed(g):
                act.wait_ge(absorbed, g + 1)
                wait_count(act, wl_ready, 2 * g)
                wait_count(act, wb_ready, 2 * g)
                a.activation(w_f[:, :, :, 0:KVR],
                             q_bank[:, 0:4 * KVR].rearrange("p (h a c) -> p h a c", h=2, a=2),
                             ACT.Copy).then_inc(w_copied, 1)

            act.wait_ge(ld_c, 16)
            a.activation(e_col[:, :, :], c_col[:, :, :], ACT.Exp, scale=-1.0).then_inc(e_ready, 1)
            for b in range(B):
                act.wait_ge(var_ready, b + 1)
                a.activation(sd[:, QT * b:QT * b + QT], sd[:, QT * b:QT * b + QT], ACT.Sqrt).then_inc(sd_ready, 1)
            act.wait_ge(modc_ready, 1)
            for b in range(B):
                for c in range(2, HC):
                    modulate(b, c, ps[4 * b + c], xt_done, HC * b + c + 1, 0, ht_ready[b])
            copy_absorbed(0)

            def squares(b):
                act.wait_ge(tok_copied, b + 1)
                for t in range(QT):
                    tt = QT * b + t
                    a.activation(junk[:, tt, 0:QR], tok[:, tt, 0:QR], ACT.Square, accum_out=ssq[:, tt, 0:1])
                    last = a.activation(junk[:, tt, QR:QR + KVR], tok[:, tt, 2 * P:2 * P + KVR], ACT.Square,
                                        accum_out=ssq[:, tt, 1:2])
                last.then_inc(ssq_ready, 1)
                act.wait_ge(ssq_ready, b + 1)
                tiles = slice(QT * b, QT * b + QT)
                a.activation(nrm[:, tiles, :], ssq[:, tiles, :], ACT.Sqrt).then_inc(nrm_ready, 1)

            def high_parts(b):
                act.wait_ge(kq_turned, 3 * b + 1)
                a.activation(kt_hi[:, b, :], ps[0][:, :], ACT.Copy).then_inc(kqt_hi, 1)
                for j, hi in enumerate((qa_hi, qb_hi)):
                    act.wait_ge(kq_turned, 3 * b + 2 + j)
                    a.activation(hi[:, b, :], ps[1 + j][:, :], ACT.Identity,
                                 scale=gq[:, j:j + 1]).then_inc(kqt_hi, 1)

            squares(0)
            high_parts(0)
            squares(1)

            def step(it):
                for slot in range(TILES):
                    if isinstance(it, int) and it == -2 and slot == 11:
                        high_parts(1)
                    if isinstance(it, int) and it < 0:
                        if it == -2 and slot in (10, 12):
                            copy_gate(slot // 2 - 5)
                    at = item(it, slot, LEAD_EXP)
                    if at:
                        g, tile = at
                        n = TILES * g + tile
                        r = tile % 4
                        act.wait_ge(max_ready, n + 1)
                        wait_count(act, t_done, n - 3)
                        a.activation(probs[:, r, :], s_bank[tile % 2][:, :], ACT.Exp, bias=neg_max[:, r:r + 1],
                                     accum_out=row_sum[:, r:r + 1]).then_inc(exp_done, 1)
                    at = item(it, slot, LEAD_NORM)
                    if at and on_scalar(at[1]):
                        g, tile = at
                        r = tile % 4
                        act.wait_ge(rec_ready, TILES * g + tile + 1)
                        a.activation(probs[:, r, :], probs[:, r, :], ACT.Copy,
                                     scale=row_rec[:, r:r + 1]).then_inc(normed_act, 1)
                    at = item(it, slot, LEAD_Q_RAW)
                    if at and at[1] % QT == 0:
                        g, tile = at
                        n = UNITS * g + tile // QT
                        act.wait_ge(q_done, n + 1)
                        wait_count(act, rot_moved, 32 * n)
                        wait_count(act, q_added, n)
                        a.activation(q_raw[KVR:P, :], q_bank[KVR:P, :], ACT.Copy).then_inc(q_raw_ready, 1)
                    at = item(it, slot, LEAD_T)
                    if at:
                        g, tile = at
                        u, t = unit_of(tile)
                        if t == 0:
                            wait_count(act, pv_done, UNITS * g + u - 1)
                        act.wait_ge(t_done, TILES * g + tile + 1)
                        a.activation(pt_hi[:, u % 2, :, t * P:(t + 1) * P],
                                     t_bank[tile % 2][:, :].rearrange("p (j q) -> p j q", q=P),
                                     ACT.Copy).then_inc(t_hi_ready, 1)
                    at = item(it, slot, LEAD_X)
                    if at and at[1] % QT == QT - 1:
                        g, tile = at
                        u, _ = unit_of(tile)
                        hl, b = head_batch(u)
                        act.wait_ge(pv_done, UNITS * g + u + 1)
                        a.activation(x_low[half(hl), b, :], pv_bank[u % 2][KVR:P, :], ACT.Copy).then_inc(x_low_ready, 1)
                    at = item(it, slot, LEAD_VO - 3)
                    if at and at[1] == 0:
                        g, _ = at
                        act.wait_ge(vo_done, g + 1)
                        a.activation(m_hi[:, :], out_bank[:, :], ACT.Copy).then_inc(m_hi_ready, 1)
                    at = item(it, slot, LEAD_ABSORB)
                    if at and at[1] == 0 and not is_first(at):
                        copy_absorbed(at[0])
                    at = item(it, slot, LEAD_X_HI)
                    if at and at[1] % QT == QT - 1 and at[1] // QT >= B:
                        g, tile = at
                        hl, b = head_batch(tile // QT)
                        act.wait_ge(x_ready, UNITS * g + tile // QT + 1)
                        act.wait_ge(o_done, TT * g + QT * (b + 1))
                        a.activation(x_hi[:, b, :], x_f[:, b, :], ACT.Copy).then_inc(x_hi_ready, 1)
                    at = item(it, slot, LEAD_Q_HI)
                    if at and at[1] % QT == 0:
                        g, tile = at
                        u, _ = unit_of(tile)
                        n = UNITS * g + u
                        act.wait_ge(q_added, n + 1)
                        wait_count(act, s_done, QT * (n - 1))
                        a.activation(q_hi[:, u % 2, :], q_f[:, :], ACT.Copy).then_inc(q_hi_ready, 1)

            run_steps(act, step)

            for k in range(TT + 2):
                if k < TT:
                    act.wait_ge(var2_ready, k + 1)
                    a.activation(sd[:, k:k + 1], sd[:, k:k + 1], ACT.Sqrt).then_inc(sd2_ready, 1)
                if 0 <= k - 2 < TT:
                    tt = k - 2
                    b, t = divmod(tt, QT)
                    act.wait_ge(xt2_done, 2 * tt + 2)
                    for c in range(HC // 2, HC):
                        a.activation(h_t[:, b, c, t * P:(t + 1) * P], turn_banks(tt)[1][:, (c - 2) * P:(c - 1) * P],
                                     ACT.Identity, scale=modc[:, 2, c, b:b + 1],
                                     bias=modc[:, 3, c, b:b + 1]).then_inc(ht2_second, 1)
                if k < TT:
                    act.wait_ge(rs2_ready, k + 1)
                    a.activation(acc[:, k, :], xs[:, k, :], ACT.Identity, scale=rs[:, k:k + 1],
                                 bias=sd[:, k:k + 1]).then_inc(xn2_ready, 1)
                if k in (1, 2):
                    copy_gate(B + k - 1)

        @block.gpsimd
        def _(pool):
            gp = nc.gpsimd
            chain = [0]

            def link(ins):
                chain[0] += 1
                ins.then_inc(pool_step, 1)
                pool.wait_ge(pool_step, chain[0])

            link(gp.memset(one[:, :], 1.0))
            gp.memset(q_rot[:, :], 0.0).then_inc(rot_clear, 1)
            pool.wait_ge(xt_done, TT)
            gp.memset(acc[:, :, :], 0.0).then_inc(acc_zero, 1)

            def step(it):
                for slot in range(TILES):
                    at = item(it, slot, LEAD_EXP)
                    if at and not on_scalar(at[1]):
                        g, tile = at
                        r = tile % 4
                        pool.wait_ge(rec_ready, TILES * g + tile + 1)
                        gp.tensor_tensor(probs[:, r, :], probs[:, r, :],
                                         row_rec[:, r:r + 1].broadcast_to((P, S)), ALU.mult).then_inc(normed, 1)
                    at = item(it, slot, LEAD_ROPE)
                    if at and at[1] % QT == 0:
                        g, tile = at
                        n = UNITS * g + tile // QT
                        pool.wait_ge(rot_moved, 32 * (n + 1))
                        gp.tensor_tensor(q_rot[:, :], q_rot[:, :], ropeq[:, 1, :],
                                         ALU.mult).then_inc(q_rotated, 1)
                        pool.wait_ge(q_rotated, n + 1)
                        pool.wait_ge(q_cos_ready, n + 1)
                        gp.tensor_tensor(q_f[:, :], q_f[:, :], q_rot[:, :],
                                         ALU.add).then_inc(q_added, 1)
                    at = item(it, slot, LEAD_Q_LO)
                    if at and at[1] % QT == 0:
                        g, tile = at
                        u, _ = unit_of(tile)
                        pool.wait_ge(q_hi_ready, UNITS * g + u + 1)
                        gp.tensor_tensor(q_lo[:, u % 2, :], q_f[:, :], q_hi[:, u % 2, :].bitcast(fp32),
                                         ALU.subtract).then_inc(q_lo_ready, 1)
                    at = item(it, slot, LEAD_X_LO)
                    if at and at[1] % QT == QT - 1 and at[1] // QT >= B:
                        g, tile = at
                        b = tile // QT % B
                        pool.wait_ge(x_hi_ready, B * g + b + 1)
                        gp.tensor_tensor(x_lo[:, b, :], x_f[:, b, :], x_hi[:, b, :].bitcast(fp32),
                                         ALU.subtract).then_inc(x_lo_ready, 1)
                    for hl in range(2):
                        at = item(it, slot, LEAD_SPLIT - 4 * hl)
                        if at and at[1] == 0:
                            g, _ = at
                            if hl == 0:
                                pool.wait_ge(w_copied, g + 1)
                                pool.wait_ge(ld_wq, 48 * (g + 1))
                            wait_count(pool, q_done, UNITS * (g - 1) + 2 * hl + 2)
                            gp.tensor_tensor(wh[:, hl, :, :].rearrange("p a c -> p (a c)"),
                                             w_f[:, hl, :, :].rearrange("p a c -> p (a c)"),
                                             one[:, :].broadcast_to((P, 2 * P)), ALU.mult).then_inc(wh_done, 1)
                            pool.wait_ge(wh_done, 2 * g + hl + 1)
                            gp.tensor_tensor(wl[:, hl, :], w_f[:, hl, 0, :], wh[:, hl, 0, :].bitcast(fp32),
                                             ALU.subtract).then_inc(wl_ready, 1)

            run_steps(pool, step)

            for k in range(TT + 6):
                if k < TT:
                    pool.wait_ge(att_gated, k + 1)
                    gp.tensor_tensor(xs[:, k, :], xs[:, k, :], acc[:, k, :], ALU.add).then_inc(res_ready, 1)
                if k == 5:
                    pool.wait_ge(att_gates_ready, 1)
                    pool.wait_ge(ffn_gates_ready, 1)
                    pool.wait_ge(ld_small, 16 * 5)
                    for b in range(B):
                        last = gp.tensor_tensor(gate_bias[:, b, :], gates[:, 1, b, :], bias_b[:, :], ALU.mult)
                    link(last)
                if 0 <= k - 5 < TT:
                    tt = k - 5
                    pool.wait_ge(xn2_ready, tt + 1)
                    gp.tensor_tensor(xs[:, tt, :], xs[:, tt, :], gate_bias[:, tt // QT, :],
                                     ALU.add).then_inc(xb_ready, 1)
                if 0 <= k - 6 < TT:
                    tt = k - 6
                    pool.wait_ge(y_gated, tt + 1)
                    pool.wait_ge(xb_ready, tt + 1)
                    gp.tensor_tensor(acc[:, tt, :], acc[:, tt, :], xs[:, tt, :], ALU.add).then_inc(y_ready, 1)


def rope_tables():
    exponent = np.arange(0, RD, 2, dtype=np.float32) / np.float32(RD)
    inv_freq = np.float32(1.0) / np.power(10000.0, exponent.astype(np.float64)).astype(np.float32)
    angle = np.outer(np.arange(S, dtype=np.float32), inv_freq).astype(np.float32).astype(np.float64)
    cos = np.concatenate([np.cos(angle)] * 2, -1)
    sin = np.concatenate([-np.sin(angle), np.sin(angle)], -1)
    on_q = np.zeros((P, 2, S), np.float64)
    on_q[:KVR, 0] = SCALING
    on_q[KVR:, 0], on_q[KVR:, 1] = cos.T * SCALING, sin.T * SCALING
    on_k = np.stack([cos, sin]).reshape(2, QT, P, RD).transpose(2, 0, 1, 3)
    return on_q.astype(np.float32), np.ascontiguousarray(on_k.astype(np.float32))


def kernel(**inputs):
    import concourse.bacc as bacc
    from concourse.bass_utils import run_bass_kernel_spmd as run

    a = {name[3:]: np.asarray(value) for name, value in inputs.items()}
    w_qa = a["attn_w_qa"]
    w_qb = a["attn_w_qb"].reshape(QR, NH, ND + RD)
    w_kvb = a["attn_w_kvb"].reshape(KVR, NH, ND + VD)
    rows = np.r_[0:QR, P:QR]
    nope_t = w_qb[rows, :, :ND].transpose(1, 2, 0)
    w_k_t = w_kvb[:, :, :ND].transpose(1, 2, 0)
    w_v_t = w_kvb[:, :, ND:].transpose(1, 2, 0)
    rope = w_qb[rows, :, ND:].reshape(2, P, NH, RD).transpose(2, 1, 0, 3)
    w_o = a["attn_w_o"].reshape(NH, VD, H)

    def pairs(t):
        return t.reshape(PAIRS, 2, *t.shape[1:]).swapaxes(1, 2)

    w_v = np.zeros((PAIRS, P, 2, P), np.float32)
    for hl in range(2):
        w_v[:, :, hl, hl * KVR:(hl + 1) * KVR] = w_v_t[hl::2]
    rope_q, rope_k = rope_tables()
    g_qa = a["attn_g_qa"]
    arrays = {
        "x": a["attn_hidden_states"],
        "w_lat": np.concatenate([w_qa, a["attn_w_kva"]], 1),
        "g_lat_q": np.stack([g_qa[:P], np.tile(g_qa[P:], 2)], 1),
        "g_lat_k": a["attn_g_kva"],
        "wq_pack": pairs(np.concatenate([nope_t, w_k_t], -1)),
        "rope_pack": pairs(rope),
        "wo_pack": np.concatenate([w_v, pairs(w_o)], -1),
        "lora_a": a["ffn_lora_A"].reshape(P, H),
        "lora_b": a["ffn_lora_B"].transpose(0, 2, 1).reshape(P, H),
        "lora_w": np.repeat(a["ffn_lora_weights"], P // a["ffn_lora_weights"].shape[0])[:, None],
        "w_ffn_t": a["ffn_W"].T,
        "bias": a["ffn_bias"],
        "c_t": a["c"].T,
        "w_mod": a["wmod"],
        "ident_in": np.eye(P, dtype=np.float32),
        "rope_q": rope_q,
        "rope_k": rope_k,
    }
    arrays = {f"in_{name}": np.ascontiguousarray(value) for name, value in arrays.items()}
    nc = bacc.Bacc("TRN2", target_bir_lowering=False, num_devices=1)
    args = [nc.dram_tensor(name, value.shape, mybir.dt.from_np(value.dtype), kind="ExternalInput").ap()
            for name, value in arrays.items()]
    out = nc.dram_tensor("out", (B, S, H), mybir.dt.float32, kind="ExternalOutput").ap()
    build(nc, *args, out)
    return run(nc, [arrays], core_ids=[0]).results[0]["out"]
```

```python
from contextlib import ExitStack

import numpy as np

import concourse.bass as bass
from concourse import mybir

B, S, H = 2, 512, 512
NH = 32
QR, KVR, RD, ND, VD = 192, 64, 64, 128, 128
P = 128
QT = S // P
TT = B * QT
HC = H // P
QRB = QR - P
PAIRS = NH // 2
UNITS = 2 * B
TILES = UNITS * QT
LP = QR + KVR + RD
LW = LP + QRB
WQ_COLS = 2 * P + KVR
WO_COLS = P + H
SCALING = (ND + RD) ** -0.5
EPS_LN, EPS_RMS = 1e-5, 1e-6
SHIFT_A, SCALE_A, GATE_A, SHIFT_B, SCALE_B, GATE_B = range(6)

LEAD_LOAD_WQ = 36
LEAD_ABSORB = 29
LEAD_SPLIT = 28
LEAD_Q = 24
LEAD_Q_RAW = 23
LEAD_Q_COS = 22
LEAD_ROPE = 22
LEAD_Q_HI = 21
LEAD_Q_LO = 20
LEAD_S = 18
LEAD_EXP = 17
LEAD_NORM = 16
LEAD_T = 15
LEAD_LOW = 14
LEAD_LOAD_WO = 13
LEAD_PV = 11
LEAD_X = 10
LEAD_X_HI = 9
LEAD_X_LO = 8
LEAD_VO = 1
OUT_SLOTS = (5, 6, 7, 9, 10, 11, 13, 14)
LORA_SLOTS = (8, 10, 12, 14)
WARM_UP = 40
RAMP = 3


def build(nc, x, w_lat, g_lat_q, g_lat_k, wq_pack, rope_pack, wo_pack, lora_a, lora_b, lora_w,
          w_ffn_t, bias, c_t, w_mod, ident_in, rope_q, rope_k, out):
    fp32 = mybir.dt.float32
    f32r = mybir.dt.float32r
    ALU = mybir.AluOpType
    ACT = mybir.ActivationFunctionType
    AX_X = mybir.AxisListType.X

    x_v = x.rearrange("b (t p) d -> p b t d", p=P)
    out_v = out.rearrange("b (t p) d -> p (b t) d", p=P)
    w_mod_v = w_mod.rearrange("(c p) (s n) -> s p c n", p=P, s=6)

    ctx = ExitStack()
    with ctx:
        def sb(name, shape, dt=fp32, where=ctx):
            return where.enter_context(nc.sbuf_tensor(name, shape, dt))

        def sem(name):
            return ctx.enter_context(nc.semaphore(name))

        xs = sb("xs", [P, TT, H])
        acc = sb("acc", [P, TT, H])
        h_t = sb("h_t", [P, B, HC, S])
        ident = sb("ident", [P, P])
        ropeq = sb("ropeq", [P, 2, S])
        ropek = sb("ropek", [P, 2, QT, RD])
        gq = sb("gq", [P, 2])
        gk = sb("gk", [P, KVR])
        gates = sb("gates", [P, 2, B, H])
        modc = sb("modc", [P, 4, HC, B])
        stats = sb("stats", [P, TT, 6])
        mv = sb("mv", [P, TT, 2])
        sd = sb("sd", [P, TT])
        rs = sb("rs", [P, TT])
        w_eff = sb("w_eff", [P, HC, H])
        bias_b = sb("bias_b", [P, H])
        kt_hi = sb("kt_hi", [P, B, S], f32r)
        kt_lo = sb("kt_lo", [P, B, S], f32r)
        kc = sb("kc", [P, B, QT, P], f32r)
        qa_hi = sb("qa_hi", [P, B, S], f32r)
        qa_lo = sb("qa_lo", [P, B, S], f32r)
        qb_hi = sb("qb_hi", [P, B, S], f32r)
        qb_lo = sb("qb_lo", [P, B, S], f32r)

        first = ExitStack()
        w_l = sb("w_l", [P, HC, LP], where=first)
        tok = sb("tok", [P, TT, LW], where=first)
        kp = sb("kp", [P, TT, P], where=first)
        c_col = sb("c_col", [P, HC, B], where=first)
        e_col = sb("e_col", [P, HC, B], where=first)
        spare = 3 * QT * S - (HC * LP + TT * LW + TT * P + 2 * HC * B)
        sb("spare", [P, spare], where=first)
        wm = sb("wm", [P, 4, HC, H], where=first)
        first.close()
        wm_gate = sb("wm_gate", [P, HC, H], where=first)
        first.close()

        pt_hi = sb("pt_hi", [P, 2, QT, S], f32r)
        pt_lo = sb("pt_lo", [P, 2, QT, S], f32r)
        x_low = sb("x_low", [P, B, S])
        x_f = sb("x_f", [P, B, S])
        x_hi = sb("x_hi", [P, B, S], f32r)
        x_lo = sb("x_lo", [P, B, S], f32r)
        m_hi = sb("m_hi", [P, H], f32r)
        m_lo = sb("m_lo", [P, H], f32r)
        wo_in = sb("wo_in", [P, 2, WO_COLS])
        probs = sb("probs", [P, 4, S])
        q_raw = sb("q_raw", [P, S])
        q_rot = sb("q_rot", [P, S])
        q_f = sb("q_f", [P, S])
        q_hi = sb("q_hi", [P, 2, S], f32r)
        q_lo = sb("q_lo", [P, 2, S], f32r)
        wq_in = sb("wq_in", [P, 2, WQ_COLS])
        w_f = sb("w_f", [P, 2, 2, P])
        wh = sb("wh", [P, 2, 2, P], f32r)
        wl = sb("wl", [P, 2, P], f32r)
        s_col = sb("s_col", [P, HC, B])
        s_pad = sb("s_pad", [P, HC, B, 32])
        one = sb("one", [P, 1])
        neg_max = sb("neg_max", [P, 4])
        row_sum = sb("row_sum", [P, 4])
        row_rec = sb("row_rec", [P, 4])
        gate_row = sb("gate_row", [P, 2, B, H])
        lora_a_sb = sb("lora_a_sb", [P, H])
        lora_b_sb = sb("lora_b_sb", [P, H])
        lora_w_sb = sb("lora_w_sb", [P, 1])
        ssq = sb("ssq", [P, TT, 2])
        nrm = sb("nrm", [P, TT, 2])
        gate_bias = gate_row[:, 0]
        mod_row = [gates[0:B, 1, place, :] for place in range(2)]
        junk = gate_row[:, :, :, :].rearrange("p k b (h n) -> p (k b h) n", h=2)
        k_rot = sb("k_rot", [P, QT, RD])

        ps = [ctx.enter_context(nc.psum_tensor(f"ps{i}", [P, S], fp32)) for i in range(8)]
        s_bank, t_bank = ps[0:2], ps[2:4]
        pv_bank = ps[4:6]
        out_bank = ps[6]
        q_bank = ps[7]

        ld_x = [sem(f"ld_x{b}") for b in range(B)]
        ld_ident, ld_c, ld_wl, ld_small, ld_lora = (sem(n) for n in ("ld_ident", "ld_c", "ld_wl", "ld_small", "ld_lora"))
        ld_mod = [sem(f"ld_mod{i}") for i in range(6)]
        ld_wq, ld_wo, rot_moved, stored = (sem(n) for n in ("ld_wq", "ld_wo", "rot_moved", "stored"))
        ve, pool_step = sem("ve"), sem("pool_step")
        var_ready, sd_ready, xn_ready, xt_done = (sem(n) for n in ("var_ready", "sd_ready", "xn_ready", "xt_done"))
        e_ready, silu_ready, pad_ready, modc_ready = (
            sem(n) for n in ("e_ready", "silu_ready", "pad_ready", "modc_ready"))
        mod_rows_done, mod_rows_copied, mod_turned = (sem(n) for n in ("mod_rows_done", "mod_rows_copied", "mod_turned"))
        ht_ready = [sem(f"ht_ready{b}") for b in range(B)]
        tok_done, tok_copied, ssq_ready, nrm_ready = (sem(n) for n in ("tok_done", "tok_copied", "ssq_ready", "nrm_ready"))
        kq_ready, kq_turned, kqt_hi, kqt_lo, kc_ready = (sem(n) for n in ("kq_ready", "kq_turned", "kqt_hi", "kqt_lo", "kc_ready"))
        gate_done, gate_copied, gate_rows_ready, att_gates_ready, ffn_gates_ready, lora_b_ready, lora_done, w_eff_ready = (
            sem(n) for n in ("gate_done", "gate_copied", "gate_rows_ready", "att_gates_ready", "ffn_gates_ready",
                             "lora_b_ready", "lora_done", "w_eff_ready"))
        acc_zero, att_gated, res_ready, xb_ready, ffn_done, y_gated, y_ready = (
            sem(n) for n in ("acc_zero", "att_gated", "res_ready", "xb_ready", "ffn_done", "y_gated", "y_ready"))
        xn2_ready, xt2_done, ht2_first, ht2_second, var2_ready, sd2_ready, rs2_ready = (
            sem(n) for n in ("xn2_ready", "xt2_done", "ht2_first", "ht2_second", "var2_ready", "sd2_ready",
                             "rs2_ready"))
        absorbed, w_copied, wh_done, wl_ready, wb_ready, rot_clear = (
            sem(n) for n in ("absorbed", "w_copied", "wh_done", "wl_ready", "wb_ready", "rot_clear"))
        q_done, q_raw_ready, q_cos_ready, q_rotated, q_added, q_hi_ready, q_lo_ready = (
            sem(n) for n in ("q_done", "q_raw_ready", "q_cos_ready", "q_rotated", "q_added", "q_hi_ready", "q_lo_ready"))
        s_done, max_ready, exp_done, rec_ready, normed, normed_act = (
            sem(n) for n in ("s_done", "max_ready", "exp_done", "rec_ready", "normed", "normed_act"))
        t_done, t_hi_ready, t_lo_ready, pv_done, x_low_ready, x_ready, x_hi_ready, x_lo_ready = (
            sem(n) for n in ("t_done", "t_hi_ready", "t_lo_ready", "pv_done", "x_low_ready", "x_ready", "x_hi_ready",
                             "x_lo_ready"))
        vo_done, m_hi_ready, m_lo_ready, o_done, o_added = (
            sem(n) for n in ("vo_done", "m_hi_ready", "m_lo_ready", "o_done", "o_added"))

        block = ctx.enter_context(nc.Block())

        def item(it, slot, lead, per_step=TILES):
            ahead, local = divmod(slot + lead, per_step)
            step = it + ahead
            if isinstance(step, int) and not 0 <= step < PAIRS:
                return None
            return step, local

        def is_first(at):
            return isinstance(at[0], int) and at[0] == 0

        def wait_count(eng, semaphore, count):
            if not isinstance(count, int) or count > 0:
                eng.wait_ge(semaphore, count)

        def run_steps(eng, step):
            for it in range(-RAMP, 0):
                step(it)
            with eng.Fori(0, PAIRS - RAMP) as it:
                step(it)
            for it in range(PAIRS - RAMP, PAIRS):
                step(it)

        def finish_gate(engine, link, kind):
            gate, mag = (gate_row[0:B * 32, kind, place, :] for place in range(2))
            engine.tensor_scalar(mag, mag, 0.25, None, ALU.max)
            link(engine.tensor_scalar(gate, gate, 0.0, None, ALU.is_ge))
            link(engine.tensor_scalar(gate, gate, 2.0, -1.0, ALU.mult, ALU.add))
            return engine.tensor_tensor(gate, gate, mag, ALU.mult)

        def last_out_bank(tt):
            return (ps[6], ps[0], ps[4], ps[5])[tt % 4]

        turn_bank = ps[1:3]

        def ffn_bank(tt):
            return (ps[3], ps[7])[tt % 2]

        def gate_bank(kind):
            return (ps[4], ps[3])[kind]

        def unit_of(tile):
            return tile // QT, tile % QT

        def head_batch(u):
            return divmod(u, B)

        def half(hl):
            return slice(hl * KVR, (hl + 1) * KVR)

        def on_scalar(tile):
            return tile % QT == QT - 1

        def normed_by(tile, g):
            before = sum(on_scalar(k) == on_scalar(tile) for k in range(tile + 1))
            each = TILES // QT if on_scalar(tile) else TILES - TILES // QT
            return (normed_act if on_scalar(tile) else normed), each * g + before

        @block.sync
        def _(sp):
            def load_wq(g):
                sp.dma_start(wq_in[:, :, :], wq_pack[g]).then_inc(ld_wq, 16)
                for ab in range(2):
                    sp.dma_start(w_f[:, :, ab, KVR:P], rope_pack[g][:, :, ab]).then_inc(ld_wq, 16)

            sp.dma_start(c_col[:, :, :], c_t.rearrange("(c p) b -> p c b", p=P)).then_inc(ld_c, 16)
            sp.dma_start(ident[:, :], ident_in).then_inc(ld_ident, 16)
            sp.dma_start(xs[:, 0:QT, :], x_v[:, 0]).then_inc(ld_x[0], 16)
            sp.dma_start(wm[:, 0], w_mod_v[SCALE_A]).then_inc(ld_mod[SCALE_A], 16)
            sp.dma_start(wm[:, 1], w_mod_v[SHIFT_A]).then_inc(ld_mod[SHIFT_A], 16)
            sp.dma_start(w_l[:, :, :], w_lat.rearrange("(c p) n -> p c n", p=P)).then_inc(ld_wl, 16)
            sp.dma_start(xs[:, QT:TT, :], x_v[:, 1]).then_inc(ld_x[1], 16)
            load_wq(0)
            sp.dma_start(ropek[:, :, :, :], rope_k).then_inc(ld_small, 16)
            sp.dma_start(ropeq[:, :, :], rope_q).then_inc(ld_small, 16)
            sp.dma_start(gq[:, :], g_lat_q).then_inc(ld_small, 16)
            sp.dma_start(gk[:, :], g_lat_k.partition_broadcast(P)).then_inc(ld_small, 16)
            sp.dma_start(bias_b[:, :], bias.partition_broadcast(P)).then_inc(ld_small, 16)
            sp.dma_start(wm[:, 3], w_mod_v[GATE_A]).then_inc(ld_mod[GATE_A], 16)
            sp.wait_ge(mod_rows_done, 1)
            sp.dma_start(wm[:, 0], w_mod_v[SHIFT_B]).then_inc(ld_mod[SHIFT_B], 16)
            sp.dma_start(wm[:, 2], w_mod_v[SCALE_B]).then_inc(ld_mod[SCALE_B], 16)
            sp.dma_start(lora_a_sb[:, :], lora_a).then_inc(ld_lora, 16)
            sp.dma_start(lora_b_sb[:, :], lora_b).then_inc(ld_lora, 16)
            sp.dma_start(lora_w_sb[:, :], lora_w).then_inc(ld_lora, 16)
            sp.dma_start(w_eff[:, :, :], w_ffn_t.rearrange("(c p) n -> p c n", p=P)).then_inc(ld_lora, 16)

            def step(it):
                for slot in range(TILES):
                    at = item(it, slot, LEAD_LOAD_WQ)
                    if at and at[1] == 0 and not is_first(at):
                        g, _ = at
                        wait_count(sp, wl_ready, 2 * g)
                        wait_count(sp, wb_ready, 2 * g)
                        load_wq(g)
                    at = item(it, slot, LEAD_LOAD_WO)
                    if at and at[1] == 0:
                        g, _ = at
                        wait_count(sp, vo_done, g)
                        if is_first(at):
                            sp.wait_ge(gate_done, 1)
                        sp.dma_start(wo_in[:, :, :], wo_pack[g]).then_inc(ld_wo, 16)
                    at = item(it, slot, LEAD_Q_RAW)
                    if at and at[1] % QT == 0:
                        g, tile = at
                        n = UNITS * g + tile // QT
                        sp.wait_ge(q_raw_ready, n + 1)
                        sp.dma_start(q_rot[64:96, :], q_raw[96:128, :]).then_inc(rot_moved, 16)
                        sp.dma_start(q_rot[96:128, :], q_raw[64:96, :]).then_inc(rot_moved, 16)

            sp.wait_ge(rot_clear, 1)
            run_steps(sp, step)
            sp.wait_ge(pv_done, UNITS * PAIRS - 1)
            sp.dma_start(wm_gate[:, :, :], w_mod_v[GATE_B]).then_inc(ld_mod[GATE_B], 16)
            for tt in range(TT):
                sp.wait_ge(y_ready, tt + 1)
                sp.dma_start(out_v[:, tt, :], acc[:, tt, :]).then_inc(stored, 16)
            sp.wait_ge(stored, 16 * TT)

        @block.tensor
        def _(pe):
            mm = nc.tensor.matmul

            def turn_x(b, ready, count, done, banks):
                pe.wait_ge(ready, count)
                for c in range(HC):
                    for t in range(QT):
                        last = nc.tensor.transpose(banks[c][:, t * P:(t + 1) * P],
                                                   acc[:, QT * b + t, c * P:(c + 1) * P], ident[:, :])
                    last.then_inc(done, 1)

            def mod_rows(bank, buf, section, chunks=range(HC)):
                pe.wait_ge(ld_mod[section], 16)
                for k in chunks:
                    last = mm(bank[0:B, :], s_col[:, k, :], wm[:, buf, k, :], start=(k == 0), stop=(k == HC - 1))
                if k == HC - 1:
                    last.then_inc(mod_rows_done, 1)

            def turn_mod_rows(bank):
                for place in range(2):
                    for n in range(HC):
                        col = (place * HC + n) * B
                        last = nc.tensor.transpose(bank[:, col:col + B], mod_row[place][:, n * P:(n + 1) * P],
                                                   ident[0:B, 0:B])
                last.then_inc(mod_turned, 1)

            def absorb():
                for hl in range(2):
                    for ab in range(2):
                        col = (2 * hl + ab) * KVR
                        last = mm(q_bank[:, col:col + KVR], wq_in[:, hl, ab * P:(ab + 1) * P],
                                  wq_in[:, hl, 2 * P:WQ_COLS], start=True, stop=True)
                last.then_inc(absorbed, 1)

            def turn_latents(b):
                pe.wait_ge(kq_ready, b + 1)
                for j in range(3):
                    for t in range(QT):
                        tt = QT * b + t
                        src = kp[:, tt, :] if j == 0 else tok[:, tt, (j - 1) * P:j * P]
                        last = nc.tensor.transpose(ps[j][:, t * P:(t + 1) * P], src, ident[:, :])
                    last.then_inc(kq_turned, 1)

            pe.wait_ge(ld_ident, 16)
            for _ in range(WARM_UP):
                nc.tensor.transpose(ps[4][:, 0:P], ident[:, :], ident[:, :])
            pe.wait_ge(silu_ready, 1)
            mod_rows(ps[7], 0, SCALE_A)
            turn_x(0, xn_ready, QT, xt_done, ps[0:4])
            mod_rows(ps[6], 1, SHIFT_A)
            pe.wait_ge(mod_rows_copied, 2)
            turn_mod_rows(ps[5])
            pe.wait_ge(ld_wl, 16)
            for b in range(B):
                pe.wait_ge(ht_ready[b], HC)
                if b:
                    pe.wait_ge(ld_wq, 48)
                    absorb()
                for t in range(QT):
                    tt = QT * b + t
                    if tt == 1:
                        pe.wait_ge(modc_ready, 1)
                        turn_x(1, xn_ready, TT, xt_done, ps[4:8])
                    if tt == TT - 1:
                        pe.wait_ge(w_copied, 1)
                    for c in range(HC):
                        last = mm(ps[tt][:, 0:LP], h_t[:, b, c, t * P:(t + 1) * P], w_l[:, c, :],
                                  start=(c == 0), stop=(c == HC - 1))
                    last.then_inc(tok_done, 1)
            turn_latents(0)
            pe.wait_ge(tok_copied, B)
            pe.wait_ge(kqt_lo, 3)
            pe.nop().then_inc(o_done, TT)

            def project(it, m, bank):
                b, t = divmod(m, QT)
                if m == 0:
                    pe.wait_ge(m_lo_ready, it + 1)
                if t == 0:
                    pe.wait_ge(x_hi_ready, B * it + b + 1)
                    pe.wait_ge(x_lo_ready, B * it + b + 1)
                cols = slice(t * P, (t + 1) * P)
                mm(bank[:, :], x_lo[:, b, cols], m_hi[:, :], start=True, stop=False)
                mm(bank[:, :], x_hi[:, b, cols], m_lo[:, :], start=False, stop=False)
                mm(bank[:, :], x_hi[:, b, cols], m_hi[:, :], start=False, stop=True).then_inc(o_done, 1)

            def gate_half(kind, weights, odd):
                for k in range(odd * HC // 2, (odd + 1) * HC // 2):
                    last = mm(gate_bank(kind)[0:B * 32, :], s_pad[:, k, :, :].rearrange("p b n -> p (b n)"),
                              weights[:, k, :], start=(k == 0), stop=(k == HC - 1))
                if odd:
                    last.then_inc(gate_done, 1)

            def ramp_work(it, slot):
                if it == -2 and slot == 11:
                    turn_latents(1)
                if it == -2 and slot == 12:
                    pe.wait_ge(kqt_lo, 6)
                    pe.wait_ge(kc_ready, B)
                if it == -2 and slot in (9, 10):
                    if slot == 9:
                        pe.wait_ge(ld_mod[GATE_A], 16)
                        pe.wait_ge(pad_ready, 1)
                    gate_half(0, wm[:, 3], slot - 9)
                if it == -2 and slot >= 14:
                    mod_rows(out_bank, 0, SHIFT_B, range(2 * slot - 28, 2 * slot - 26))
                if it == -1 and slot in (1, 2):
                    pe.wait_ge(mod_rows_copied, 3)
                    mod_rows(out_bank, 2, SCALE_B, range(2 * slot - 2, 2 * slot))
                if it == -1 and slot == 4:
                    pe.wait_ge(mod_rows_copied, 4)
                    turn_mod_rows(out_bank)
                if it == -1 and slot in LORA_SLOTS:
                    c = LORA_SLOTS.index(slot)
                    if c == 0:
                        pe.wait_ge(lora_b_ready, 1)
                        pe.wait_ge(modc_ready, 2)
                    else:
                        pe.wait_ge(w_eff_ready, c)
                    mm(out_bank[:, :], lora_a_sb[:, c * P:(c + 1) * P], lora_b_sb[:, :],
                       start=True, stop=True).then_inc(lora_done, 1)

            def step(it):
                for slot in range(TILES):
                    if isinstance(it, int):
                        ramp_work(it, slot)
                    at = item(it, slot, LEAD_T)
                    if at:
                        g, tile = at
                        n = TILES * g + tile
                        pe.wait_ge(*normed_by(tile, g))
                        wait_count(pe, t_hi_ready, n - 1)
                        wait_count(pe, t_lo_ready, n - 1)
                        for j in range(QT):
                            last = nc.tensor.transpose(t_bank[tile % 2][:, j * P:(j + 1) * P],
                                                       probs[:, tile % 4, j * P:(j + 1) * P], ident[:, :])
                        last.then_inc(t_done, 1)

                    at = item(it, slot, LEAD_S)
                    if at:
                        g, tile = at
                        n = TILES * g + tile
                        u, t = unit_of(tile)
                        if t == 0:
                            pe.wait_ge(q_hi_ready, UNITS * g + u + 1)
                            pe.wait_ge(q_lo_ready, UNITS * g + u + 1)
                        wait_count(pe, exp_done, n - 1)
                        bank, cols, b = s_bank[tile % 2], slice(t * P, (t + 1) * P), head_batch(u)[1]
                        mm(bank[:, :], q_lo[:, u % 2, cols], kt_hi[:, b, :], start=True, stop=False)
                        mm(bank[:, :], q_hi[:, u % 2, cols], kt_lo[:, b, :], start=False, stop=False)
                        mm(bank[:, :], q_hi[:, u % 2, cols], kt_hi[:, b, :], start=False,
                           stop=True).then_inc(s_done, 1)

                    at = item(it, slot, LEAD_ABSORB)
                    if at and at[1] == 0 and not is_first(at):
                        g, _ = at
                        pe.wait_ge(ld_wq, 48 * (g + 1))
                        wait_count(pe, q_cos_ready, UNITS * (g - 1) + UNITS - 1)
                        absorb()

                    at = item(it, slot, LEAD_Q)
                    if at and at[1] % QT == 0:
                        g, tile = at
                        u, _ = unit_of(tile)
                        n = UNITS * g + u
                        hl, b = head_batch(u)
                        if b == 0:
                            pe.wait_ge(wl_ready, 2 * g + hl + 1)
                            pe.wait_ge(wb_ready, 2 * g + hl + 1)
                        if u == UNITS - 1:
                            pe.wait_ge(w_copied, min(g + 2, PAIRS) if isinstance(g, int) else g + 2)
                        else:
                            wait_count(pe, q_cos_ready, n)
                        mm(q_bank[:, :], wl[:, hl, :], qa_hi[:, b, :], start=True, stop=False)
                        mm(q_bank[:, :], wh[:, hl, 0, :], qa_lo[:, b, :], start=False, stop=False)
                        mm(q_bank[:, :], wh[0:QRB, hl, 1, :], qb_lo[0:QRB, b, :], start=False, stop=False)
                        mm(q_bank[:, :], wh[:, hl, 1, :], qb_hi[:, b, :], start=False, stop=False)
                        mm(q_bank[:, :], wh[:, hl, 0, :], qa_hi[:, b, :], start=False,
                           stop=True).then_inc(q_done, 1)

                    at = item(it, slot, LEAD_PV)
                    if at:
                        g, tile = at
                        u, t = unit_of(tile)
                        n = UNITS * g + u
                        if t == 0:
                            pe.wait_ge(t_hi_ready, QT * n + QT)
                            wait_count(pe, x_ready, n - 1)
                        if t == QT // 2:
                            pe.wait_ge(t_lo_ready, QT * n + QT)
                        part = pt_hi if t < QT // 2 else pt_lo
                        for j in (2 * t % QT, 2 * t % QT + 1):
                            last = mm(pv_bank[u % 2][:, :], kc[:, head_batch(u)[1], j, :], part[:, u % 2, j, :],
                                      start=(t == 0 and j == 0), stop=(t == QT - 1 and j == QT - 1))
                        if t == QT - 1:
                            last.then_inc(pv_done, 1)

                    if slot in OUT_SLOTS and item(it, slot, 0) and not (isinstance(it, int) and it == PAIRS - 1):
                        m = OUT_SLOTS.index(slot)
                        if m:
                            pe.wait_ge(o_added, TT + TT * it + m)
                        project(it, m, out_bank)

                    for hl in range(2):
                        at = item(it, slot, LEAD_VO - 2 * hl)
                        if at and at[1] == 0:
                            g, _ = at
                            if hl == 0:
                                pe.wait_ge(ld_wo, 16 * (g + 1))
                                pe.wait_ge(o_added, TT + TT * g)
                                if is_first(at):
                                    pe.wait_ge(w_eff_ready, HC)
                            last = mm(out_bank[:, :], wo_in[:, hl, 0:P], wo_in[:, hl, P:WO_COLS],
                                      start=(hl == 0), stop=(hl == 1))
                            if hl == 1:
                                last.then_inc(vo_done, 1)

            run_steps(pe, step)

            def last_project(k):
                if k >= 4:
                    pe.wait_ge(o_added, TT + TT * (PAIRS - 1) + k - 3)
                elif k == 3:
                    pe.wait_ge(x_ready, UNITS * PAIRS)
                project(PAIRS - 1, k, last_out_bank(k))

            for k in range(4):
                last_project(k)
            pe.wait_ge(ld_mod[GATE_B], 16)
            for odd in range(2):
                gate_half(1, wm_gate, odd)
            for k in range(TT + 1):
                if k < TT:
                    pe.wait_ge(xn2_ready, k + 1)
                    if k >= 1:
                        pe.wait_ge(ht2_first, HC // 2 * k)
                        pe.wait_ge(ht2_second, HC // 2 * k)
                    for c in range(HC):
                        last = nc.tensor.transpose(turn_bank[c // 2][:, c % 2 * P:(c % 2 + 1) * P],
                                                   acc[:, k, c * P:(c + 1) * P], ident[:, :])
                        if c % 2:
                            last.then_inc(xt2_done, 1)
                if k + 4 < TT:
                    last_project(k + 4)
                if k >= 1:
                    tt = k - 1
                    b, t = divmod(tt, QT)
                    pe.wait_ge(ht2_first, HC // 2 * (tt + 1))
                    pe.wait_ge(ht2_second, HC // 2 * (tt + 1))
                    if tt == 0:
                        pe.wait_ge(w_eff_ready, HC)
                        pe.wait_ge(gate_copied, 4)
                    if tt >= 2:
                        pe.wait_ge(y_gated, tt - 1)
                    for c in range(HC):
                        last = mm(ffn_bank(tt)[:, :], h_t[:, b, c, t * P:(t + 1) * P], w_eff[:, c, :],
                                  start=(c == 0), stop=(c == HC - 1))
                    last.then_inc(ffn_done, 1)

        @block.vector
        def _(dve):
            v = nc.vector
            chain = [0]

            def link(ins):
                chain[0] += 1
                ins.then_inc(ve, 1)
                dve.wait_ge(ve, chain[0])

            def statistics(b):
                tiles = range(QT * b, QT * b + QT)
                dve.wait_ge(ld_x[b], 16)
                for tt in tiles:
                    last = v.bn_stats(stats[:, tt, :], xs[:, tt, :])
                link(last)
                for tt in tiles:
                    last = v.bn_aggr(mv[:, tt, :], stats[:, tt, :])
                link(last)
                span = slice(QT * b, QT * b + QT)
                v.tensor_scalar(sd[:, span], mv[:, span, 1], EPS_LN, None, ALU.add).then_inc(var_ready, 1)

            def normalise(b):
                span = slice(QT * b, QT * b + QT)
                dve.wait_ge(sd_ready, b + 1)
                link(v.reciprocal(rs[:, span], sd[:, span]))
                for tt in range(QT * b, QT * b + QT):
                    v.tensor_scalar(acc[:, tt, :], xs[:, tt, :], mv[:, tt, 0:1], rs[:, tt:tt + 1],
                                    ALU.subtract, ALU.mult).then_inc(xn_ready, 1)

            def modulate(b, c, bank, turned, count, kind, done):
                dve.wait_ge(turned, count)
                v.tensor_scalar(h_t[:, b, c, :], bank[:, :], modc[:, 2 * kind, c, b:b + 1],
                                modc[:, 2 * kind + 1, c, b:b + 1], ALU.mult, ALU.add).then_inc(done, 1)

            link(v.memset(s_pad[:, :, :, :], 0.0))
            dve.wait_ge(ld_c, 16)
            dve.wait_ge(e_ready, 1)
            link(v.tensor_scalar(s_col[:, :, :], e_col[:, :, :], 1.0, None, ALU.add))
            link(v.reciprocal(e_col[:, :, :], s_col[:, :, :]))
            v.tensor_tensor(s_col[:, :, :], c_col[:, :, :], e_col[:, :, :], ALU.mult).then_inc(silu_ready, 1)
            statistics(0)
            normalise(0)
            dve.wait_ge(silu_ready, 1)
            v.tensor_copy(s_pad[:, :, :, 0], s_col[:, :, :]).then_inc(pad_ready, 1)
            statistics(1)
            dve.wait_ge(mod_turned, 1)
            v.tensor_scalar(modc[:, 0], ps[5][:, 0:HC * B].rearrange("p (n b) -> p n b", b=B), 1.0, None, ALU.add)
            link(v.tensor_copy(modc[:, 1], ps[5][:, HC * B:2 * HC * B].rearrange("p (n b) -> p n b", b=B)))
            v.nop().then_inc(modc_ready, 1)
            for c in range(2):
                modulate(0, c, ps[c], xt_done, c + 1, 0, ht_ready[0])
            normalise(1)
            for c in range(2):
                modulate(1, c, ps[4 + c], xt_done, HC + c + 1, 0, ht_ready[1])
            dve.wait_ge(ld_small, 16 * 5)

            def copy_tokens(b):
                for t in range(QT):
                    tt = QT * b + t
                    dve.wait_ge(tok_done, tt + 1)
                    v.tensor_copy(tok[:, tt, 0:QR], ps[tt][:, 0:QR])
                    last = v.tensor_copy(tok[:, tt, QR:LW], ps[tt][:, P:LP])
                last.then_inc(tok_copied, 1)

            def latents(b):
                tiles = slice(QT * b, QT * b + QT)
                dve.wait_ge(tok_copied, b + 1)
                kr = tok[:, tiles, 2 * P + KVR:LW]
                v.tensor_tensor(kp[:, tiles, KVR:P], kr, ropek[:, 0], ALU.mult)
                v.tensor_tensor(k_rot[:, :, 0:RD // 2], kr[:, :, RD // 2:RD], ropek[:, 1, :, 0:RD // 2], ALU.mult)
                link(v.tensor_tensor(k_rot[:, :, RD // 2:RD], kr[:, :, 0:RD // 2], ropek[:, 1, :, RD // 2:RD], ALU.mult))
                v.tensor_tensor(kp[:, tiles, KVR:P], kp[:, tiles, KVR:P], k_rot[:, :, :], ALU.add)
                dve.wait_ge(nrm_ready, b + 1)
                v.tensor_scalar(nrm[:, tiles, 0], nrm[:, tiles, 0], QR ** -0.5, EPS_RMS, ALU.mult, ALU.add)
                link(v.tensor_scalar(nrm[:, tiles, 1], nrm[:, tiles, 1], KVR ** -0.5, EPS_RMS, ALU.mult, ALU.add))
                link(v.reciprocal(ssq[:, tiles, :], nrm[:, tiles, :]))
                for tt in range(QT * b, QT * b + QT):
                    v.scalar_tensor_tensor(kp[:, tt, 0:KVR], tok[:, tt, 2 * P:2 * P + KVR], ssq[:, tt, 1:2],
                                           gk[:, :], ALU.mult, ALU.mult)
                for tt in range(QT * b, QT * b + QT):
                    last = v.tensor_scalar(tok[:, tt, 0:2 * P], tok[:, tt, 0:2 * P], ssq[:, tt, 0:1], None, ALU.mult)
                last.then_inc(kq_ready, 1)
                dve.wait_ge(kq_ready, b + 1)
                link(v.tensor_copy(kc[:, b, :, 0:KVR], kp[:, tiles, 0:KVR]))
                v.tensor_tensor(kc[:, b, :, KVR:P], kp[:, tiles, 0:KVR], kc[:, b, :, 0:KVR].bitcast(fp32),
                                ALU.subtract).then_inc(kc_ready, 1)

            def low_parts(b):
                dve.wait_ge(kqt_hi, 3 * b + 1)
                v.tensor_tensor(kt_lo[:, b, :], ps[0][:, :], kt_hi[:, b, :].bitcast(fp32),
                                ALU.subtract).then_inc(kqt_lo, 1)
                for j, (hi, lo) in enumerate(((qa_hi, qa_lo), (qb_hi, qb_lo))):
                    dve.wait_ge(kqt_hi, 3 * b + 2 + j)
                    v.scalar_tensor_tensor(lo[:, b, :], ps[1 + j][:, :], gq[:, j:j + 1],
                                           hi[:, b, :].bitcast(fp32), ALU.mult, ALU.subtract).then_inc(kqt_lo, 1)

            copy_tokens(0)
            latents(0)
            copy_tokens(1)
            low_parts(0)
            dve.wait_ge(ld_lora, 16 * 4)
            v.tensor_scalar(lora_b_sb[:, :], lora_b_sb[:, :], lora_w_sb[:, 0:1], 2.0, ALU.mult,
                            ALU.mult).then_inc(lora_b_ready, 1)

            v.nop().then_inc(o_added, TT)

            def ramp_work(it, slot):
                if it == -2 and slot == 6:
                    latents(1)
                if it == -2 and slot == 11:
                    low_parts(1)
                if it == -2 and slot == 13:
                    dve.wait_ge(gate_copied, 2)
                    finish_gate(v, link, 0).then_inc(gate_rows_ready, 1)
                if it == -1 and slot == 5:
                    dve.wait_ge(mod_turned, 2)
                    v.tensor_scalar(modc[:, 2], out_bank[:, 0:HC * B].rearrange("p (n b) -> p n b", b=B),
                                    1.0, None, ALU.add)
                    link(v.tensor_copy(modc[:, 3], out_bank[:, HC * B:2 * HC * B].rearrange("p (n b) -> p n b", b=B)))
                    v.nop().then_inc(modc_ready, 1)
                if it == -1 and slot - 1 in LORA_SLOTS:
                    c = LORA_SLOTS.index(slot - 1)
                    dve.wait_ge(lora_done, c + 1)
                    v.tensor_tensor(w_eff[:, c, :], out_bank[:, :], w_eff[:, c, :], ALU.add).then_inc(w_eff_ready, 1)

            def step(it):
                for slot in range(TILES):
                    if isinstance(it, int):
                        ramp_work(it, slot)
                    if slot - 1 in OUT_SLOTS and item(it, slot, 0) and not (isinstance(it, int) and it == PAIRS - 1):
                        m = OUT_SLOTS.index(slot - 1)
                        dve.wait_ge(o_done, TT + TT * it + m + 1)
                        if m == 0 and isinstance(it, int):
                            dve.wait_ge(acc_zero, 1)
                        v.tensor_tensor(acc[:, m, :], out_bank[:, :], acc[:, m, :], ALU.add).then_inc(o_added, 1)
                    at = item(it, slot, LEAD_LOW)
                    if at:
                        g, tile = at
                        u, t = unit_of(tile)
                        dve.wait_ge(t_hi_ready, TILES * g + tile + 1)
                        v.tensor_tensor(pt_lo[:, u % 2, :, t * P:(t + 1) * P],
                                        t_bank[tile % 2][:, :].rearrange("p (j q) -> p j q", q=P),
                                        pt_hi[:, u % 2, :, t * P:(t + 1) * P].bitcast(fp32),
                                        ALU.subtract).then_inc(t_lo_ready, 1)
                    at = item(it, slot, LEAD_EXP)
                    if at:
                        g, tile = at
                        dve.wait_ge(exp_done, TILES * g + tile + 1)
                        v.reciprocal(row_rec[:, tile % 4:tile % 4 + 1],
                                     row_sum[:, tile % 4:tile % 4 + 1]).then_inc(rec_ready, 1)
                    at = item(it, slot, LEAD_S)
                    if at:
                        g, tile = at
                        dve.wait_ge(s_done, TILES * g + tile + 1)
                        v.reduce_max(neg_max[:, tile % 4:tile % 4 + 1], s_bank[tile % 2][:, :], AX_X,
                                     negate=True).then_inc(max_ready, 1)
                    at = item(it, slot, LEAD_Q_COS)
                    if at and at[1] % QT == 0:
                        g, tile = at
                        n = UNITS * g + tile // QT
                        dve.wait_ge(q_raw_ready, n + 1)
                        wait_count(dve, q_hi_ready, n)
                        wait_count(dve, q_lo_ready, n)
                        v.tensor_tensor(q_f[:, :], q_bank[:, :], ropeq[:, 0, :], ALU.mult).then_inc(q_cos_ready, 1)
                    at = item(it, slot, LEAD_X)
                    if at and at[1] % QT == QT - 1:
                        g, tile = at
                        u, _ = unit_of(tile)
                        hl, b = head_batch(u)
                        dve.wait_ge(x_low_ready, UNITS * g + u + 1)
                        if hl == 0:
                            wait_count(dve, x_lo_ready, B * (g - 1) + b + 1)
                        v.tensor_tensor(x_f[half(hl), b, :], pv_bank[u % 2][0:KVR, :], x_low[half(hl), b, :],
                                        ALU.add).then_inc(x_ready, 1)
                    at = item(it, slot, LEAD_VO - 4)
                    if at and at[1] == 0:
                        g, _ = at
                        dve.wait_ge(m_hi_ready, g + 1)
                        v.tensor_tensor(m_lo[:, :], out_bank[:, :], m_hi[:, :].bitcast(fp32),
                                        ALU.subtract).then_inc(m_lo_ready, 1)
                    for hl in range(2):
                        at = item(it, slot, LEAD_SPLIT - 1 - 4 * hl)
                        if at and at[1] == 0:
                            g, _ = at
                            dve.wait_ge(wh_done, 2 * g + hl + 1)
                            v.tensor_tensor(wh[QRB:P, hl, 1, :], w_f[QRB:P, hl, 1, :],
                                            wh[QRB:P, hl, 1, :].bitcast(fp32), ALU.subtract).then_inc(wb_ready, 1)

            run_steps(dve, step)

            for k in range(TT + 4):
                if k < TT:
                    tt = k
                    dve.wait_ge(o_done, TT + TT * (PAIRS - 1) + tt + 1)
                    if tt == 0:
                        dve.wait_ge(att_gates_ready, B)
                    v.tensor_tensor(acc[:, tt, :], last_out_bank(tt)[:, :], acc[:, tt, :], ALU.add).then_inc(o_added, 1)
                    dve.wait_ge(o_added, TT + TT * (PAIRS - 1) + tt + 1)
                    v.tensor_tensor(acc[:, tt, :], acc[:, tt, :], gates[:, 0, tt // QT, :],
                                    ALU.mult).then_inc(att_gated, 1)
                if 0 <= k - 1 < TT:
                    tt = k - 1
                    dve.wait_ge(res_ready, tt + 1)
                    link(v.bn_stats(stats[:, tt, :], xs[:, tt, :]))
                    link(v.bn_aggr(mv[:, tt, :], stats[:, tt, :]))
                    v.tensor_scalar(sd[:, tt:tt + 1], mv[:, tt, 1:2], EPS_LN, None, ALU.add).then_inc(var2_ready, 1)
                if 0 <= k - 1 < TT:
                    tt = k - 1
                    dve.wait_ge(sd2_ready, tt + 1)
                    link(v.reciprocal(rs[:, tt:tt + 1], sd[:, tt:tt + 1]))
                    v.scalar_tensor_tensor(sd[:, tt:tt + 1], mv[:, tt, 0:1], -1.0, rs[:, tt:tt + 1],
                                           ALU.mult, ALU.mult).then_inc(rs2_ready, 1)
                if 0 <= k - 2 < TT:
                    tt = k - 2
                    b, t = divmod(tt, QT)
                    dve.wait_ge(xt2_done, 2 * tt + 1)
                    for c in range(HC // 2):
                        v.tensor_scalar(h_t[:, b, c, t * P:(t + 1) * P], turn_bank[0][:, c * P:(c + 1) * P],
                                        modc[:, 2, c, b:b + 1], modc[:, 3, c, b:b + 1],
                                        ALU.mult, ALU.add).then_inc(ht2_first, 1)
                if k == 3:
                    dve.wait_ge(gate_copied, 4)
                    finish_gate(v, link, 1).then_inc(gate_rows_ready, 1)
                if 0 <= k - 4 < TT:
                    tt = k - 4
                    dve.wait_ge(ffn_done, tt + 1)
                    if tt == 0:
                        dve.wait_ge(ffn_gates_ready, B)
                    v.tensor_tensor(acc[:, tt, :], ffn_bank(tt)[:, :], gates[:, 1, tt // QT, :],
                                    ALU.mult).then_inc(y_gated, 1)

        @block.scalar
        def _(act):
            a = nc.scalar

            def modulate(b, c, bank, turned, count, kind, done):
                act.wait_ge(turned, count)
                a.activation(h_t[:, b, c, :], bank[:, :], ACT.Identity, scale=modc[:, 2 * kind, c, b:b + 1],
                             bias=modc[:, 2 * kind + 1, c, b:b + 1]).then_inc(done, 1)

            def copy_gate(kind):
                act.wait_ge(gate_done, kind + 1)
                for place, func in enumerate((ACT.Copy, ACT.Abs)):
                    a.activation(gate_row[0:B * 32, kind, place, :], gate_bank(kind)[0:B * 32, :],
                                 func).then_inc(gate_copied, 1)

            def copy_absorbed(g):
                act.wait_ge(absorbed, g + 1)
                wait_count(act, wl_ready, 2 * g)
                wait_count(act, wb_ready, 2 * g)
                a.activation(w_f[:, :, :, 0:KVR],
                             q_bank[:, 0:4 * KVR].rearrange("p (h a c) -> p h a c", h=2, a=2),
                             ACT.Copy).then_inc(w_copied, 1)

            act.wait_ge(ld_c, 16)
            a.activation(e_col[:, :, :], c_col[:, :, :], ACT.Exp, scale=-1.0).then_inc(e_ready, 1)
            def copy_mod_row(i, bank, place):
                act.wait_ge(mod_rows_done, i)
                a.activation(mod_row[place], bank[0:B, :], ACT.Copy).then_inc(mod_rows_copied, 1)

            for b in range(B):
                act.wait_ge(var_ready, b + 1)
                a.activation(sd[:, QT * b:QT * b + QT], sd[:, QT * b:QT * b + QT], ACT.Sqrt).then_inc(sd_ready, 1)
                if b == 0:
                    copy_mod_row(1, ps[7], 0)
                    copy_mod_row(2, ps[6], 1)
            act.wait_ge(modc_ready, 1)
            for b in range(B):
                for c in range(2, HC):
                    modulate(b, c, ps[4 * b + c], xt_done, HC * b + c + 1, 0, ht_ready[b])
            copy_absorbed(0)

            def squares(b):
                act.wait_ge(tok_copied, b + 1)
                for t in range(QT):
                    tt = QT * b + t
                    a.activation(junk[:, tt, 0:QR], tok[:, tt, 0:QR], ACT.Square, accum_out=ssq[:, tt, 0:1])
                    last = a.activation(junk[:, tt, QR:QR + KVR], tok[:, tt, 2 * P:2 * P + KVR], ACT.Square,
                                        accum_out=ssq[:, tt, 1:2])
                last.then_inc(ssq_ready, 1)
                act.wait_ge(ssq_ready, b + 1)
                tiles = slice(QT * b, QT * b + QT)
                a.activation(nrm[:, tiles, :], ssq[:, tiles, :], ACT.Sqrt).then_inc(nrm_ready, 1)

            def high_parts(b):
                act.wait_ge(kq_turned, 3 * b + 1)
                a.activation(kt_hi[:, b, :], ps[0][:, :], ACT.Copy).then_inc(kqt_hi, 1)
                for j, hi in enumerate((qa_hi, qb_hi)):
                    act.wait_ge(kq_turned, 3 * b + 2 + j)
                    a.activation(hi[:, b, :], ps[1 + j][:, :], ACT.Identity,
                                 scale=gq[:, j:j + 1]).then_inc(kqt_hi, 1)

            squares(0)
            high_parts(0)
            squares(1)

            def step(it):
                for slot in range(TILES):
                    if isinstance(it, int) and it == -2 and slot == 11:
                        high_parts(1)
                    if isinstance(it, int) and it < 0:
                        if (it, slot) in ((-1, 0), (-1, 3)):
                            copy_mod_row(3 + slot // 3, out_bank, 1 - slot // 3)
                        if it == -2 and slot == 11:
                            copy_gate(0)
                    at = item(it, slot, LEAD_EXP)
                    if at:
                        g, tile = at
                        n = TILES * g + tile
                        r = tile % 4
                        act.wait_ge(max_ready, n + 1)
                        wait_count(act, t_done, n - 3)
                        a.activation(probs[:, r, :], s_bank[tile % 2][:, :], ACT.Exp, bias=neg_max[:, r:r + 1],
                                     accum_out=row_sum[:, r:r + 1]).then_inc(exp_done, 1)
                    at = item(it, slot, LEAD_NORM)
                    if at and on_scalar(at[1]):
                        g, tile = at
                        r = tile % 4
                        act.wait_ge(rec_ready, TILES * g + tile + 1)
                        a.activation(probs[:, r, :], probs[:, r, :], ACT.Copy,
                                     scale=row_rec[:, r:r + 1]).then_inc(normed_act, 1)
                    at = item(it, slot, LEAD_Q_RAW)
                    if at and at[1] % QT == 0:
                        g, tile = at
                        n = UNITS * g + tile // QT
                        act.wait_ge(q_done, n + 1)
                        wait_count(act, rot_moved, 32 * n)
                        wait_count(act, q_added, n)
                        a.activation(q_raw[KVR:P, :], q_bank[KVR:P, :], ACT.Copy).then_inc(q_raw_ready, 1)
                    at = item(it, slot, LEAD_T)
                    if at:
                        g, tile = at
                        u, t = unit_of(tile)
                        if t == 0:
                            wait_count(act, pv_done, UNITS * g + u - 1)
                        act.wait_ge(t_done, TILES * g + tile + 1)
                        a.activation(pt_hi[:, u % 2, :, t * P:(t + 1) * P],
                                     t_bank[tile % 2][:, :].rearrange("p (j q) -> p j q", q=P),
                                     ACT.Copy).then_inc(t_hi_ready, 1)
                    at = item(it, slot, LEAD_X)
                    if at and at[1] % QT == QT - 1:
                        g, tile = at
                        u, _ = unit_of(tile)
                        hl, b = head_batch(u)
                        act.wait_ge(pv_done, UNITS * g + u + 1)
                        a.activation(x_low[half(hl), b, :], pv_bank[u % 2][KVR:P, :], ACT.Copy).then_inc(x_low_ready, 1)
                    at = item(it, slot, LEAD_VO - 3)
                    if at and at[1] == 0:
                        g, _ = at
                        act.wait_ge(vo_done, g + 1)
                        a.activation(m_hi[:, :], out_bank[:, :], ACT.Copy).then_inc(m_hi_ready, 1)
                    at = item(it, slot, LEAD_ABSORB)
                    if at and at[1] == 0 and not is_first(at):
                        copy_absorbed(at[0])
                    at = item(it, slot, LEAD_X_HI)
                    if at and at[1] % QT == QT - 1 and at[1] // QT >= B:
                        g, tile = at
                        hl, b = head_batch(tile // QT)
                        act.wait_ge(x_ready, UNITS * g + tile // QT + 1)
                        act.wait_ge(o_done, TT * g + QT * (b + 1))
                        a.activation(x_hi[:, b, :], x_f[:, b, :], ACT.Copy).then_inc(x_hi_ready, 1)
                    at = item(it, slot, LEAD_Q_HI)
                    if at and at[1] % QT == 0:
                        g, tile = at
                        u, _ = unit_of(tile)
                        n = UNITS * g + u
                        act.wait_ge(q_added, n + 1)
                        wait_count(act, s_done, QT * (n - 1))
                        a.activation(q_hi[:, u % 2, :], q_f[:, :], ACT.Copy).then_inc(q_hi_ready, 1)

            run_steps(act, step)

            for k in range(TT + 1):
                if k < TT:
                    act.wait_ge(var2_ready, k + 1)
                    a.activation(sd[:, k:k + 1], sd[:, k:k + 1], ACT.Sqrt).then_inc(sd2_ready, 1)
                if k < TT:
                    act.wait_ge(rs2_ready, k + 1)
                    a.activation(acc[:, k, :], xs[:, k, :], ACT.Identity, scale=rs[:, k:k + 1],
                                 bias=sd[:, k:k + 1]).then_inc(xn2_ready, 1)
                if 0 <= k - 1 < TT:
                    tt = k - 1
                    b, t = divmod(tt, QT)
                    act.wait_ge(xt2_done, 2 * tt + 2)
                    for c in range(HC // 2, HC):
                        a.activation(h_t[:, b, c, t * P:(t + 1) * P], turn_bank[1][:, (c - 2) * P:(c - 1) * P],
                                     ACT.Identity, scale=modc[:, 2, c, b:b + 1],
                                     bias=modc[:, 3, c, b:b + 1]).then_inc(ht2_second, 1)
                if k == 1:
                    copy_gate(1)

        @block.gpsimd
        def _(pool):
            gp = nc.gpsimd
            chain = [0]

            def link(ins):
                chain[0] += 1
                ins.then_inc(pool_step, 1)
                pool.wait_ge(pool_step, chain[0])

            link(gp.memset(one[:, :], 1.0))
            gp.memset(q_rot[:, :], 0.0).then_inc(rot_clear, 1)
            pool.wait_ge(xt_done, TT)
            gp.memset(acc[:, :, :], 0.0).then_inc(acc_zero, 1)

            def spread_gates(kind, done):
                pool.wait_ge(gate_rows_ready, kind + 1)
                link(gp.nop())
                for b in range(B):
                    gp.partition_broadcast(gates[:, kind, b, :], gate_row[32 * b:32 * b + 1, kind, 0, :]).then_inc(done, 1)
                    pool.wait_ge(done, b + 1)

            def step(it):
                for slot in range(TILES):
                    if isinstance(it, int) and it == -1 and slot == 1:
                        spread_gates(0, att_gates_ready)
                    at = item(it, slot, LEAD_EXP)
                    if at and not on_scalar(at[1]):
                        g, tile = at
                        r = tile % 4
                        pool.wait_ge(rec_ready, TILES * g + tile + 1)
                        gp.tensor_tensor(probs[:, r, :], probs[:, r, :],
                                         row_rec[:, r:r + 1].broadcast_to((P, S)), ALU.mult).then_inc(normed, 1)
                    at = item(it, slot, LEAD_ROPE)
                    if at and at[1] % QT == 0:
                        g, tile = at
                        n = UNITS * g + tile // QT
                        pool.wait_ge(rot_moved, 32 * (n + 1))
                        gp.tensor_tensor(q_rot[:, :], q_rot[:, :], ropeq[:, 1, :],
                                         ALU.mult).then_inc(q_rotated, 1)
                        pool.wait_ge(q_rotated, n + 1)
                        pool.wait_ge(q_cos_ready, n + 1)
                        gp.tensor_tensor(q_f[:, :], q_f[:, :], q_rot[:, :],
                                         ALU.add).then_inc(q_added, 1)
                    at = item(it, slot, LEAD_Q_LO)
                    if at and at[1] % QT == 0:
                        g, tile = at
                        u, _ = unit_of(tile)
                        pool.wait_ge(q_hi_ready, UNITS * g + u + 1)
                        gp.tensor_tensor(q_lo[:, u % 2, :], q_f[:, :], q_hi[:, u % 2, :].bitcast(fp32),
                                         ALU.subtract).then_inc(q_lo_ready, 1)
                    at = item(it, slot, LEAD_X_LO)
                    if at and at[1] % QT == QT - 1 and at[1] // QT >= B:
                        g, tile = at
                        b = tile // QT % B
                        pool.wait_ge(x_hi_ready, B * g + b + 1)
                        gp.tensor_tensor(x_lo[:, b, :], x_f[:, b, :], x_hi[:, b, :].bitcast(fp32),
                                         ALU.subtract).then_inc(x_lo_ready, 1)
                    for hl in range(2):
                        at = item(it, slot, LEAD_SPLIT - 4 * hl)
                        if at and at[1] == 0:
                            g, _ = at
                            if hl == 0:
                                pool.wait_ge(w_copied, g + 1)
                                pool.wait_ge(ld_wq, 48 * (g + 1))
                            wait_count(pool, q_done, UNITS * (g - 1) + 2 * hl + 2)
                            gp.tensor_tensor(wh[:, hl, :, :].rearrange("p a c -> p (a c)"),
                                             w_f[:, hl, :, :].rearrange("p a c -> p (a c)"),
                                             one[:, :].broadcast_to((P, 2 * P)), ALU.mult).then_inc(wh_done, 1)
                            pool.wait_ge(wh_done, 2 * g + hl + 1)
                            gp.tensor_tensor(wl[:, hl, :], w_f[:, hl, 0, :], wh[:, hl, 0, :].bitcast(fp32),
                                             ALU.subtract).then_inc(wl_ready, 1)

            run_steps(pool, step)

            for k in range(TT + 5):
                if k < TT:
                    pool.wait_ge(att_gated, k + 1)
                    gp.tensor_tensor(xs[:, k, :], xs[:, k, :], acc[:, k, :], ALU.add).then_inc(res_ready, 1)
                if k == 3:
                    spread_gates(1, ffn_gates_ready)
                if k == 4:
                    pool.wait_ge(att_gates_ready, B)
                    pool.wait_ge(ffn_gates_ready, B)
                    pool.wait_ge(ld_small, 16 * 5)
                    for b in range(B):
                        last = gp.tensor_tensor(gate_bias[:, b, :], gates[:, 1, b, :], bias_b[:, :], ALU.mult)
                    link(last)
                if 0 <= k - 4 < TT:
                    tt = k - 4
                    pool.wait_ge(xn2_ready, tt + 1)
                    gp.tensor_tensor(xs[:, tt, :], xs[:, tt, :], gate_bias[:, tt // QT, :],
                                     ALU.add).then_inc(xb_ready, 1)
                if 0 <= k - 5 < TT:
                    tt = k - 5
                    pool.wait_ge(y_gated, tt + 1)
                    pool.wait_ge(xb_ready, tt + 1)
                    gp.tensor_tensor(acc[:, tt, :], acc[:, tt, :], xs[:, tt, :], ALU.add).then_inc(y_ready, 1)


def rope_tables():
    exponent = np.arange(0, RD, 2, dtype=np.float32) / np.float32(RD)
    inv_freq = np.float32(1.0) / np.power(10000.0, exponent.astype(np.float64)).astype(np.float32)
    angle = np.outer(np.arange(S, dtype=np.float32), inv_freq).astype(np.float32).astype(np.float64)
    cos = np.concatenate([np.cos(angle)] * 2, -1)
    sin = np.concatenate([-np.sin(angle), np.sin(angle)], -1)
    on_q = np.zeros((P, 2, S), np.float64)
    on_q[:KVR, 0] = SCALING
    on_q[KVR:, 0], on_q[KVR:, 1] = cos.T * SCALING, sin.T * SCALING
    on_k = np.stack([cos, sin]).reshape(2, QT, P, RD).transpose(2, 0, 1, 3)
    return on_q.astype(np.float32), np.ascontiguousarray(on_k.astype(np.float32))


def kernel(**inputs):
    import concourse.bacc as bacc
    from concourse.bass_utils import run_bass_kernel_spmd as run

    a = {name[3:]: np.asarray(value) for name, value in inputs.items()}
    w_qa = a["attn_w_qa"]
    w_qb = a["attn_w_qb"].reshape(QR, NH, ND + RD)
    w_kvb = a["attn_w_kvb"].reshape(KVR, NH, ND + VD)
    rows = np.r_[0:QR, P:QR]
    nope_t = w_qb[rows, :, :ND].transpose(1, 2, 0)
    w_k_t = w_kvb[:, :, :ND].transpose(1, 2, 0)
    w_v_t = w_kvb[:, :, ND:].transpose(1, 2, 0)
    rope = w_qb[rows, :, ND:].reshape(2, P, NH, RD).transpose(2, 1, 0, 3)
    w_o = a["attn_w_o"].reshape(NH, VD, H)

    def pairs(t):
        return t.reshape(PAIRS, 2, *t.shape[1:]).swapaxes(1, 2)

    w_v = np.zeros((PAIRS, P, 2, P), np.float32)
    for hl in range(2):
        w_v[:, :, hl, hl * KVR:(hl + 1) * KVR] = w_v_t[hl::2]
    rope_q, rope_k = rope_tables()
    g_qa = a["attn_g_qa"]
    arrays = {
        "x": a["attn_hidden_states"],
        "w_lat": np.concatenate([w_qa, a["attn_w_kva"]], 1),
        "g_lat_q": np.stack([g_qa[:P], np.tile(g_qa[P:], 2)], 1),
        "g_lat_k": a["attn_g_kva"],
        "wq_pack": pairs(np.concatenate([nope_t, w_k_t], -1)),
        "rope_pack": pairs(rope),
        "wo_pack": np.concatenate([w_v, pairs(w_o)], -1),
        "lora_a": a["ffn_lora_A"].reshape(P, H),
        "lora_b": a["ffn_lora_B"].transpose(0, 2, 1).reshape(P, H),
        "lora_w": np.repeat(a["ffn_lora_weights"], P // a["ffn_lora_weights"].shape[0])[:, None],
        "w_ffn_t": a["ffn_W"].T,
        "bias": a["ffn_bias"],
        "c_t": a["c"].T,
        "w_mod": a["wmod"],
        "ident_in": np.eye(P, dtype=np.float32),
        "rope_q": rope_q,
        "rope_k": rope_k,
    }
    arrays = {f"in_{name}": np.ascontiguousarray(value) for name, value in arrays.items()}
    nc = bacc.Bacc("TRN2", target_bir_lowering=False, num_devices=1)
    args = [nc.dram_tensor(name, value.shape, mybir.dt.from_np(value.dtype), kind="ExternalInput").ap()
            for name, value in arrays.items()]
    out = nc.dram_tensor("out", (B, S, H), mybir.dt.float32, kind="ExternalOutput").ap()
    build(nc, *args, out)
    return run(nc, [arrays], core_ids=[0]).results[0]["out"]
```
